# Optimizing a Trainium2 kernel written in Bass

```python
import numpy as np
import jax
import jax.numpy as jnp

def _softmax(x, axis=-1):
    return jax.nn.softmax(x, axis=axis)

def _gelu(x):
    return jax.nn.gelu(x, approximate=True)

def _silu(x):
    return jax.nn.silu(x)

def _sigmoid(x):
    return jax.nn.sigmoid(x)

def _layernorm(x, axis=-1, eps=1e-05):
    m = jnp.mean(x, axis=axis, keepdims=True)
    v = jnp.var(x, axis=axis, keepdims=True)
    return (x - m) / jnp.sqrt(v + eps)

def _scatter_add(tgt, idx, src, axis=0):
    return tgt.at[idx].add(src)

def _segment_sum(src, seg, n):
    return jax.ops.segment_sum(src, seg, n)
kernel_name = 'mk_hybrid_d1_jaxref_r8_2800ab'

def setup_inputs(seed: int=0):
    np.random.seed(seed)
    _w = jnp.asarray

    def _L0_attn_a_setup():
        import jax, jax.numpy as jnp
        import numpy as np
        import math
        D_MODEL, D_C, D_R, NH = (128, 128, 32, 16)
        HD = D_MODEL // NH
        B, T = (2, 256)

        def _rope_tables(T, d_R):
            inv_freq = 1.0 / 10000.0 ** (jnp.arange(0, d_R, 2, dtype=jnp.float32) / d_R)
            t = jnp.arange(T, dtype=jnp.float32)
            freqs = jnp.outer(t, inv_freq)
            return (jnp.cos(freqs), jnp.sin(freqs))

        def _rotary_apply(x, cos, sin):
            d = x.shape[-1]
            x1, x2 = (x[..., :d // 2], x[..., d // 2:])
            return jnp.concatenate([x1 * cos - x2 * sin, x2 * cos + x1 * sin], axis=-1)
        key = jax.random.key(seed)
        ks = jax.random.split(key, 8)
        s = lambda fan_in: 1.0 / math.sqrt(fan_in)
        return {'x': jax.random.normal(ks[0], (B, T, D_MODEL), jnp.float32), 'W_kv_down': jax.random.normal(ks[1], (D_MODEL, D_C), jnp.float32) * s(D_MODEL), 'W_k_up': jax.random.normal(ks[2], (D_C, D_MODEL), jnp.float32) * s(D_C), 'W_v_up': jax.random.normal(ks[3], (D_C, D_MODEL), jnp.float32) * s(D_C), 'W_q': jax.random.normal(ks[4], (D_MODEL, D_MODEL), jnp.float32) * s(D_MODEL), 'W_q_rope': jax.random.normal(ks[5], (D_MODEL, D_R), jnp.float32) * s(D_MODEL), 'W_k_rope': jax.random.normal(ks[6], (D_C, D_R), jnp.float32) * s(D_C), 'W_o': jax.random.normal(ks[7], (D_MODEL, D_MODEL), jnp.float32) * s(D_MODEL)}
    _L0_attn_a_in = _L0_attn_a_setup()

    def _L0_attn_b_setup():
        import jax, jax.numpy as jnp
        import numpy as np
        NUM_HEADS = 16
        key = jax.random.key(seed)
        kx, kq, kk, kv = jax.random.split(key, 4)
        N, S, D = (2, 512, 128)
        scale = 1.0 / np.sqrt(D)
        x = jax.random.normal(kx, (N, S, D), dtype=jnp.float32)
        Wq = jax.random.normal(kq, (D, D), dtype=jnp.float32) * scale
        Wk = jax.random.normal(kk, (D, D), dtype=jnp.float32) * scale
        Wv = jax.random.normal(kv, (D, D), dtype=jnp.float32) * scale
        return {'x': x, 'Wq': Wq, 'Wk': Wk, 'Wv': Wv}
    _L0_attn_b_in = _L0_attn_b_setup()

    def _L0_ffn_setup():
        import jax, jax.numpy as jnp
        import numpy as np
        DIM = 128
        NUM_EXPERTS = 8
        HIDDEN = 512
        CAP_FACTOR = 2.0
        B, S = (4, 256)
        key = jax.random.key(seed)
        ks = jax.random.split(key, 6)
        scale_r = 1.0 / np.sqrt(DIM)
        scale_1 = 1.0 / np.sqrt(DIM)
        scale_2 = 1.0 / np.sqrt(HIDDEN)
        return {'x': jax.random.normal(ks[0], (B, S, DIM), dtype=jnp.float32), 'router_w': jax.random.uniform(ks[1], (NUM_EXPERTS, DIM), jnp.float32, -scale_r, scale_r), 'w1': jax.random.uniform(ks[2], (NUM_EXPERTS, DIM, HIDDEN), jnp.float32, -scale_1, scale_1), 'b1': jax.random.uniform(ks[3], (NUM_EXPERTS, HIDDEN), jnp.float32, -scale_1, scale_1), 'w2': jax.random.uniform(ks[4], (NUM_EXPERTS, HIDDEN, DIM), jnp.float32, -scale_2, scale_2), 'b2': jax.random.uniform(ks[5], (NUM_EXPERTS, DIM), jnp.float32, -scale_2, scale_2)}
    _L0_ffn_in = _L0_ffn_setup()
    _d = {'L0_attn_a_x': _L0_attn_a_in['x'], 'L0_attn_a_W_kv_down': _L0_attn_a_in['W_kv_down'], 'L0_attn_a_W_k_up': _L0_attn_a_in['W_k_up'], 'L0_attn_a_W_v_up': _L0_attn_a_in['W_v_up'], 'L0_attn_a_W_q': _L0_attn_a_in['W_q'], 'L0_attn_a_W_q_rope': _L0_attn_a_in['W_q_rope'], 'L0_attn_a_W_k_rope': _L0_attn_a_in['W_k_rope'], 'L0_attn_a_W_o': _L0_attn_a_in['W_o'], 'L0_attn_b_Wq': _L0_attn_b_in['Wq'], 'L0_attn_b_Wk': _L0_attn_b_in['Wk'], 'L0_attn_b_Wv': _L0_attn_b_in['Wv'], 'L0_ffn_router_w': _L0_ffn_in['router_w'], 'L0_ffn_w1': _L0_ffn_in['w1'], 'L0_ffn_b1': _L0_ffn_in['b1'], 'L0_ffn_w2': _L0_ffn_in['w2'], 'L0_ffn_b2': _L0_ffn_in['b2']}
    _x0 = _d['L0_attn_a_x']
    _d['L0_attn_a_x'] = jax.random.normal(jax.random.fold_in(jax.random.key(seed), 1), (4, 1024, 128), dtype=_x0.dtype)
    del _x0
    return _d

def reference(L0_attn_a_x, L0_attn_a_W_kv_down, L0_attn_a_W_k_up, L0_attn_a_W_v_up, L0_attn_a_W_q, L0_attn_a_W_q_rope, L0_attn_a_W_k_rope, L0_attn_a_W_o, L0_attn_b_Wq, L0_attn_b_Wk, L0_attn_b_Wv, L0_ffn_router_w, L0_ffn_w1, L0_ffn_b1, L0_ffn_w2, L0_ffn_b2):

    def _L0_attn_a_ref(x, W_kv_down, W_k_up, W_v_up, W_q, W_q_rope, W_k_rope, W_o):
        import jax, jax.numpy as jnp
        import numpy as np
        import math
        D_MODEL, D_C, D_R, NH = (128, 128, 32, 16)
        HD = D_MODEL // NH
        B, T = (2, 256)

        def _rope_tables(T, d_R):
            inv_freq = 1.0 / 10000.0 ** (jnp.arange(0, d_R, 2, dtype=jnp.float32) / d_R)
            t = jnp.arange(T, dtype=jnp.float32)
            freqs = jnp.outer(t, inv_freq)
            return (jnp.cos(freqs), jnp.sin(freqs))

        def _rotary_apply(x, cos, sin):
            d = x.shape[-1]
            x1, x2 = (x[..., :d // 2], x[..., d // 2:])
            return jnp.concatenate([x1 * cos - x2 * sin, x2 * cos + x1 * sin], axis=-1)
        Bb, Tt, _ = x.shape
        cos, sin = _rope_tables(Tt, D_R)
        cos = cos[None]
        sin = sin[None]
        c_kv = x @ W_kv_down
        k_rope = _rotary_apply(c_kv @ W_k_rope, cos, sin)
        k = (c_kv @ W_k_up).reshape(Bb, Tt, NH, HD)
        v = (c_kv @ W_v_up).reshape(Bb, Tt, NH, HD)
        q = (x @ W_q).reshape(Bb, Tt, NH, HD)
        q_rope = _rotary_apply(x @ W_q_rope, cos, sin)
        scale = math.sqrt(HD + D_R)
        scores = jnp.einsum('bqhd,bkhd->bhqk', q, k)
        scores = scores + jnp.einsum('bqr,bkr->bqk', q_rope, k_rope)[:, None]
        scores = scores / scale
        causal = jnp.triu(jnp.ones((Tt, Tt), dtype=bool), k=1)
        scores = jnp.where(causal[None, None], -jnp.inf, scores)
        w = jax.nn.softmax(scores, axis=-1)
        attn = jnp.einsum('bhqk,bkhd->bqhd', w, v).reshape(Bb, Tt, D_MODEL)
        return attn @ W_o

    def _L0_attn_b_ref(x, Wq, Wk, Wv):
        import jax, jax.numpy as jnp
        import numpy as np
        NUM_HEADS = 16
        N, S, D = x.shape
        H = NUM_HEADS
        hd = D // H
        q = (x @ Wq.T).reshape(N, S, H, hd).transpose(0, 2, 1, 3)
        k = (x @ Wk.T).reshape(N, S, H, hd).transpose(0, 2, 1, 3)
        v = (x @ Wv.T).reshape(N, S, H, hd).transpose(0, 2, 1, 3)
        energy = jnp.einsum('nhqd,nhkd->nhqk', q, k)
        attn = jax.nn.softmax(energy / jnp.sqrt(jnp.float32(hd)), axis=3)
        out = jnp.einsum('nhql,nhld->nhqd', attn, v)
        return out.transpose(0, 2, 1, 3).reshape(N, S, D)

    def _L0_ffn_ref(x, router_w, w1, b1, w2, b2):
        import jax, jax.numpy as jnp
        import numpy as np
        DIM = 128
        NUM_EXPERTS = 8
        HIDDEN = 512
        CAP_FACTOR = 2.0
        B, S = (4, 256)
        Bz, Sz, Dz = x.shape
        E = router_w.shape[0]
        capacity = max(1, int(Sz * CAP_FACTOR / E) + 1)
        scores = jax.nn.softmax(jnp.einsum('bsd,ed->bse', x, router_w), axis=-1)
        scores_t = jnp.swapaxes(scores, 1, 2)
        gate_vals, sel_idx = jax.lax.top_k(scores_t, capacity)
        b_idx = jnp.arange(Bz)[:, None, None]
        tokens = x[b_idx, sel_idx]
        h = jnp.einsum('becd,edh->bech', tokens, w1) + b1[None, :, None, :]
        h = jax.nn.gelu(h, approximate=False)
        y = jnp.einsum('bech,ehd->becd', h, w2) + b2[None, :, None, :]
        gated = y * gate_vals[..., None]
        out = jnp.zeros_like(x).at[b_idx, sel_idx].add(gated)
        return out
    x = L0_attn_a_x
    x = x + _L0_attn_a_ref(_layernorm(x, axis=-1), L0_attn_a_W_kv_down, L0_attn_a_W_k_up, L0_attn_a_W_v_up, L0_attn_a_W_q, L0_attn_a_W_q_rope, L0_attn_a_W_k_rope, L0_attn_a_W_o)
    x = x + _L0_ffn_ref(_layernorm(x, axis=-1), L0_ffn_router_w, L0_ffn_w1, L0_ffn_b1, L0_ffn_w2, L0_ffn_b2)
    x = x + _L0_attn_b_ref(_layernorm(x, axis=-1), L0_attn_b_Wq, L0_attn_b_Wk, L0_attn_b_Wv)
    x = x + _L0_ffn_ref(_layernorm(x, axis=-1), L0_ffn_router_w, L0_ffn_w1, L0_ffn_b1, L0_ffn_w2, L0_ffn_b2)
    return x

_drawn_inputs = setup_inputs


def setup_inputs(seed=0):
    import zlib

    import numpy as np

    out = dict(_drawn_inputs(seed))
    spreads = {}
    factors = {'L0_ffn_b1': 4.55, 'L0_ffn_b2': 3.284}
    for name, (base, spread) in spreads.items():
        noise = np.random.default_rng([zlib.crc32(name.encode()), seed]).standard_normal(out[name].shape)
        drawn = base * np.exp(spread * noise) if base else spread * noise
        out[name] = jnp.asarray(drawn.astype(out[name].dtype))
    for name, factor in factors.items():
        out[name] = (out[name] * factor).astype(out[name].dtype)
    return out
```

```python
from contextlib import ExitStack

import concourse.bass as bass
from concourse import mybir

F32 = mybir.dt.float32
BF16 = mybir.dt.bfloat16
ALU = mybir.AluOpType
ACT = mybir.ActivationFunctionType
AX = mybir.AxisListType

P = 128
B, T, D = 4, 1024, 128
NC = T // P
HALF = 512
NHALF = T // HALF
CPH = HALF // P
HD = 8
GH = 4
NG = D // HD // GH
STEPS = B * NG
DR = 32
NE, HID = 8, 512
KH = HID // P
CAP = max(1, int(T * 2.0 / NE) + 1)
ROUNDS, REST = divmod(CAP, 8)
assert REST == 1
EPS = 1e-5
BIG = -1e30
PRIME = 2

PAIRS = [(0, 0), (0, 1), (1, 0), (1, 1), (0, 2), (2, 0)]
NMAXP = 3
ROPE_TILE = PAIRS[:4]
ROPE_REST = PAIRS[4:]
MROW = len(PAIRS) * HD
RROW = 64
NROW = NMAXP * DR
KMAX = NROW + NMAXP * HD


def mk_program(nc, x_in, w_kv_down, w_k_up, w_v_up, w_q, w_q_rope, w_k_rope, w_o, wq_b, wk_b, wv_b,
               router_w, w1, b1, w2, b2, cos2, sin2, out):
    ctx = ExitStack()
    with ctx:
        def sb(name, shape, dt=F32):
            return ctx.enter_context(nc.sbuf_tensor(name, shape, dt))

        def pb(name, dt=F32):
            return ctx.enter_context(nc.psum_tensor(name, [P, 2 * HALF if name.endswith("_2") else HALF], dt))

        names, fresh = [0], []

        def sem(name):
            names[0] += 1
            made = ctx.enter_context(nc.semaphore(f"{name}_{names[0]}"))
            fresh.append(made)
            return made

        def prime(e):
            for made in fresh:
                e.sem_inc(made, PRIME)
            fresh.clear()

        def until(e, semaphore, count):
            e.wait_ge(semaphore, count + PRIME)

        s_passed = sem("passed")

        def passed(e):
            e.sem_inc(s_passed, 1)

        x_sb = sb("x_sb", [P, B * NC, D])
        ident = sb("ident", [P, P])
        identb = sb("identb", [P, P], BF16)
        mask_qk = sb("mask_qk", [P, P], BF16)
        mask_kq = sb("mask_kq", [P, P], BF16)
        wa = sb("wa", [P, 5, D])
        wr = sb("wr", [P, 4, DR])
        wbn = sb("wbn", [P, 3, D])
        wbt = sb("wbt", [P, 3, D])
        cs = sb("cs", [2 * DR, 2, T])
        w1_sb = sb("w1_sb", [P, NE, HID])
        w2_sb = sb("w2_sb", [P, NE, KH, D])
        b1n = sb("b1n", [NE * KH, P])
        b1t = sb("b1t", [P, NE * KH])
        b2blk = sb("b2blk", [B * NE, B, D])
        rwn = sb("rwn", [NE, D])
        rwt = sb("rwt", [P, NE])
        rev = sb("rev", [B * NE, T])
        v_all = sb("v_all", [P, B, NG, NC, GH * HD])
        y_all = sb("y_all", [P, B, NG, NC, GH * HD])
        xnT_all = y_all[:, :, :, :, :].rearrange("p b g c d -> p b (g c d)")
        sc = sb("sc", [P, NC, B, NE])
        gate = sb("gate", [P, NC, B * NE])
        scT = sb("scT", [B * NE, T])

        def of_phase():
            own = ExitStack()
            names[0] += 1
            tag = names[0]
            return (lambda name, shape, dt=F32: own.enter_context(nc.sbuf_tensor(f"{name}_{tag}", shape, dt))), own.close

        bank = [pb(f"bank{i}") for i in range(4)]
        wide = [pb(f"wide{i}_2") for i in range(2)]

        qk_dram = nc.dram_tensor("qk_parts", [2, 3, B, P, T], BF16, kind="Internal").ap()
        rope_dram = nc.dram_tensor("rope_parts", [3, B, 2 * DR, T], BF16, kind="Internal").ap()

        def load():
            s_ld, s_b2, s_c, s_t = sem("loaded"), sem("b2_loaded"), sem("consts"), sem("turned")
            loads = [(x_sb[:, :, :], x_in.rearrange("b (c p) d -> p (b c) d", p=P))]
            loads += [(wa[:, n, :], w) for n, w in enumerate((w_q, w_kv_down, w_k_up, w_v_up, w_o))]
            for n, w in ((0, w_q_rope), (2, w_k_rope)):
                h = DR // 2
                loads += [(wr[:, n, :], w), (wr[:, n + 1, 0:h], w[:, h:DR]), (wr[:, n + 1, h:DR], w[:, 0:h])]
            loads += [(wbn[:, n, :], w) for n, w in enumerate((wq_b, wk_b, wv_b))]
            loads += [(cs[n * DR:(n + 1) * DR, i, :], t) for n in range(2) for i, t in enumerate((cos2, sin2))]
            loads += [(w1_sb[:, :, :], w1.rearrange("e p h -> p e h")),
                      (w2_sb[:, :, :, :], w2.rearrange("e (k p) d -> p e k d", p=P)),
                      (b1n[:, :], b1.rearrange("e (k p) -> (e k) p", p=P)), (rwn[:, :], router_w)]
            with nc.Block() as block:
                @block.sync
                def _(e):
                    prime(e)
                    for dst, src in loads:
                        e.dma_start(dst, src).then_inc(s_ld, 16)
                    until(e, s_c, 5)
                    for b in range(B):
                        e.dma_start(b2blk[b * NE:(b + 1) * NE, b, :], b2).then_inc(s_b2, 16)
                    until(e, s_ld, 16 * len(loads))
                    until(e, s_b2, 16 * B)

                @block.gpsimd
                def _(e):
                    for m, v in ((ident, 0.0), (identb, 0.0), (mask_qk, 0.0), (mask_kq, 0.0)):
                        e.memset(m[:, :], v).then_inc(s_c, 1)
                    e.memset(b2blk[:, :, :], 0.0).then_inc(s_c, 1)
                    until(e, s_c, 5)
                    for m in (ident, identb):
                        e.affine_select(out=m[:, :], in_=m[:, :], compare_op=ALU.not_equal, fill=1.0, base=0,
                                        pattern=[[-1, P]], channel_multiplier=1).then_inc(s_c, 1)
                    e.affine_select(out=mask_qk[:, :], in_=mask_qk[:, :], compare_op=ALU.is_ge, fill=BIG, base=0,
                                    pattern=[[-1, P]], channel_multiplier=1).then_inc(s_c, 1)
                    e.affine_select(out=mask_kq[:, :], in_=mask_kq[:, :], compare_op=ALU.is_ge, fill=BIG, base=0,
                                    pattern=[[1, P]], channel_multiplier=-1).then_inc(s_c, 1)
                    e.iota(rev[:, :], pattern=[[-1, T]], base=T, channel_multiplier=0,
                           allow_small_or_imprecise_dtypes=True).then_inc(s_c, 1)

                @block.tensor
                def _(e):
                    until(e, s_c, 7)
                    until(e, s_ld, 16 * len(loads))
                    for n in range(3):
                        e.transpose(bank[0][:, n * D:(n + 1) * D], wbn[:, n, :], ident[:, :])
                    e.transpose(bank[1][:, 0:NE * KH], b1n[:, :], ident[0:NE * KH, 0:NE * KH])
                    e.transpose(bank[1][:, 64:64 + NE], rwn[:, :], ident[0:NE, 0:NE]).then_inc(s_t, 1)

                @block.vector
                def _(e):
                    until(e, s_t, 1)
                    e.tensor_copy(wbt[:, :, :], bank[0][:, 0:3 * D].rearrange("p (n d) -> p n d", n=3))
                    e.tensor_copy(b1t[:, :], bank[1][:, 0:NE * KH])
                    e.tensor_copy(rwt[:, :], bank[1][:, 64:64 + NE])

        class Norm:

            def __init__(self, buf):
                self.buffers = (buf("xn", [P, NC, D]), buf("xnT", [P, T]), buf("stats", [P, NC, 6]),
                                buf("lnv", [P, 5, NC]))
                self.st, self.var, self.std = sem("ln_stat"), sem("ln_var"), sem("ln_std")
                self.xn, self.tr, self.ev = sem("ln_xn"), sem("ln_tr"), sem("ln_ev")
                self.ch = sem("ln_chain")

            def vector(self, e, b):
                xn, xnT, stats, lnv = self.buffers
                for c in range(NC):
                    ins = e.bn_stats(stats[:, c, :], x_sb[:, bass.ds(b * NC + c, 1), :].rearrange("p o d -> p (o d)"))
                ins.then_inc(self.ch, 1)
                me, mo = stats[:, :, 1], stats[:, :, 4]
                until(e, self.ch, b * 6 + 1)
                e.tensor_tensor(lnv[:, 0, :], me, mo, ALU.subtract).then_inc(self.ch, 1)
                e.tensor_tensor(lnv[:, 1, :], stats[:, :, 2], stats[:, :, 5], ALU.add)
                e.tensor_tensor(lnv[:, 2, :], me, mo, ALU.add).then_inc(self.ch, 1)
                until(e, self.ch, b * 6 + 3)
                e.scalar_tensor_tensor(lnv[:, 3, :], lnv[:, 0, :], 0.25, lnv[:, 0, :],
                                       ALU.mult, ALU.mult).then_inc(self.ch, 1)
                e.tensor_scalar(lnv[:, 1, :], lnv[:, 1, :], 1.0 / D, EPS, ALU.mult, ALU.add)
                e.tensor_scalar(lnv[:, 2, :], lnv[:, 2, :], 0.5, None, ALU.mult).then_inc(self.ch, 1)
                until(e, self.ch, b * 6 + 5)
                e.tensor_tensor(lnv[:, 3, :], lnv[:, 1, :], lnv[:, 3, :], ALU.add).then_inc(self.var, 1)
                until(e, self.std, b + 1)
                e.reciprocal(lnv[:, 0, :], lnv[:, 4, :]).then_inc(self.ch, 1)
                until(e, self.ch, b * 6 + 6)
                until(e, self.tr, b * NHALF)
                for c in range(NC):
                    ins = e.tensor_scalar(xn[:, c, :], x_sb[:, bass.ds(b * NC + c, 1), :].rearrange("p o d -> p (o d)"),
                                          lnv[:, 2, c:c + 1], lnv[:, 0, c:c + 1], ALU.subtract, ALU.mult)
                    if c % CPH == CPH - 1:
                        ins.then_inc(self.xn, 1)

            def scalar_std(self, e, b):
                xn, xnT, stats, lnv = self.buffers
                until(e, self.var, b + 1)
                e.activation(lnv[:, 4, :], lnv[:, 3, :], ACT.Sqrt).then_inc(self.std, 1)

            def tensor(self, e, b):
                xn, xnT, stats, lnv = self.buffers
                until(e, self.ev, b * NHALF)
                for h in range(NHALF):
                    until(e, self.xn, b * NHALF + h + 1)
                    for c in range(CPH):
                        ins = e.transpose(bank[h][:, c * P:(c + 1) * P], xn[:, h * CPH + c, :], ident[:, :])
                    ins.then_inc(self.tr, 1)

            def scalar_evac(self, e, b, free, count):
                xn, xnT, stats, lnv = self.buffers
                until(e, free, count)
                for h in range(NHALF):
                    until(e, self.tr, b * NHALF + h + 1)
                    e.activation(xnT[:, h * HALF:(h + 1) * HALF], bank[h][:, :], ACT.Copy).then_inc(self.ev, 1)

        def project(latent):
            buf, give_back = of_phase()
            ln = Norm(buf)
            xnT, cT = ln.buffers[1], buf("cT", [P, T])
            parts = buf("parts", [P, 2, 3, T], BF16)
            rparts = buf("rparts", [2 * DR, 3, T], BF16)
            resid = buf("resid", [P, 2, HALF])
            rot = buf("rot", [2 * DR, 3, HALF])
            s_mm, s_hi, s_r1, s_mid, s_lo = sem("proj"), sem("hi"), sem("resid"), sem("mid"), sem("lo")
            s_c, s_cev = sem("latent"), sem("latent_ev")
            s_rp, s_rt, s_rr, s_rhi, s_rr1, s_rmid, s_rlo = (sem(n) for n in (
                "rope", "rope_prod", "rope_rot", "rope_hi", "rope_r1", "rope_mid", "rope_lo"))
            s_v, s_vev, s_out = sem("v"), sem("v_ev"), sem("parts_out")
            wq_ = wa[:, 0, :] if latent else wbt[:, 0, :]
            wk_ = wa[:, 2, :] if latent else wbt[:, 1, :]
            wv_ = wa[:, 3, :] if latent else wbt[:, 2, :]
            kin = cT if latent else xnT
            NQ = 2 * NHALF
            dma_per_b = 2 + latent
            with nc.Block() as block:
                @block.tensor
                def _(e):
                    with e.Fori(0, B) as b:
                        ln.tensor(e, b)
                        until(e, ln.ev, b * NHALF + NHALF)
                        if latent:
                            until(e, s_cev, b * NHALF)
                            for h in range(NHALF):
                                e.matmul(wide[0][:, h * HALF:(h + 1) * HALF], wa[:, 1, :],
                                         xnT[:, h * HALF:(h + 1) * HALF], start=True, stop=True).then_inc(s_c, 1)
                            until(e, s_cev, b * NHALF + NHALF)
                        for n in range(NQ):
                            t, h = divmod(n, NHALF)
                            if n >= 2:
                                until(e, s_r1, b * NQ + n - 1)
                            else:
                                until(e, s_r1, b * NQ)
                            e.matmul(bank[2 + n % 2][:, :], wk_ if t else wq_,
                                     (kin if t else xnT)[:, h * HALF:(h + 1) * HALF],
                                     start=True, stop=True).then_inc(s_mm, 1)
                        if latent:
                            for h in range(NHALF):
                                until(e, s_rt, b * NHALF + h)
                                for sw in range(2):
                                    e.matmul(wide[1][0:DR, sw * HALF:(sw + 1) * HALF], wr[:, sw, :],
                                             xnT[:, h * HALF:(h + 1) * HALF], start=True, stop=True)
                                    ins = e.matmul(wide[1][DR:2 * DR, sw * HALF:(sw + 1) * HALF], wr[:, 2 + sw, :],
                                                   cT[:, h * HALF:(h + 1) * HALF], start=True, stop=True)
                                ins.then_inc(s_rp, 1)
                        until(e, s_vev, b * NHALF)
                        for h in range(NHALF):
                            for c in range(CPH):
                                at = h * CPH + c
                                ins = e.matmul(bank[h][:, c * D:(c + 1) * D], kin[:, at * P:(at + 1) * P], wv_,
                                               start=True, stop=True)
                            ins.then_inc(s_v, 1)
                        until(e, s_vev, b * NHALF + NHALF)

                @block.scalar
                def _(e):
                    with e.Fori(0, B) as b:
                        ln.scalar_std(e, b)
                        ln.scalar_evac(e, b, s_v, b * NHALF)
                        if latent:
                            for h in range(NHALF):
                                until(e, s_c, b * NHALF + h + 1)
                                e.activation(cT[:, h * HALF:(h + 1) * HALF], wide[0][:, h * HALF:(h + 1) * HALF],
                                             ACT.Copy).then_inc(s_cev, 1)
                        until(e, s_out, b * 16 * dma_per_b)
                        for n in range(NQ):
                            t, h = divmod(n, NHALF)
                            until(e, s_mm, b * NQ + n + 1)
                            e.activation(parts[:, t, 0, h * HALF:(h + 1) * HALF], bank[2 + n % 2][:, :],
                                         ACT.Copy).then_inc(s_hi, 1)
                        if latent:
                            for h in range(NHALF):
                                until(e, s_rr, b * NHALF + h + 1)
                                e.activation(rparts[:, 0, h * HALF:(h + 1) * HALF], rot[:, 0, :],
                                             ACT.Copy).then_inc(s_rhi, 1)
                        for h in range(NHALF):
                            until(e, s_v, b * NHALF + h + 1)
                            for c in range(CPH):
                                dst = v_all[:, bass.ds(b, 1), :, h * CPH + c, :].rearrange("p o g d -> p (o g) d")
                                ins = e.activation(dst, bank[h][:, c * D:(c + 1) * D].rearrange("p (g d) -> p g d", g=NG),
                                                   ACT.Copy)
                            ins.then_inc(s_vev, 1)

                @block.vector
                def _(e):
                    with e.Fori(0, B) as b:
                        ln.vector(e, b)
                        for n in range(NQ):
                            t, h = divmod(n, NHALF)
                            until(e, s_hi, b * NQ + n + 1)
                            if n >= 2:
                                until(e, s_lo, b * NQ + n - 1)
                            else:
                                until(e, s_lo, b * NQ)
                            e.tensor_tensor(resid[:, n % 2, :], bank[2 + n % 2][:, :],
                                            parts[:, t, 0, h * HALF:(h + 1) * HALF], ALU.subtract).then_inc(s_r1, 1)
                        if latent:
                            for h in range(NHALF):
                                until(e, s_rp, b * NHALF + h + 1)
                                until(e, s_rlo, b * NHALF + h)
                                cols = slice(h * HALF, (h + 1) * HALF)
                                e.tensor_tensor(rot[:, 1, :], wide[1][0:2 * DR, 0:HALF], cs[:, 0, cols], ALU.mult)
                                e.tensor_tensor(rot[:, 2, :], wide[1][0:2 * DR, HALF:2 * HALF], cs[:, 1, cols],
                                                ALU.mult).then_inc(s_rt, 1)
                                until(e, s_rt, b * NHALF + h + 1)
                                e.tensor_tensor(rot[:, 0, :], rot[:, 1, :], rot[:, 2, :], ALU.add).then_inc(s_rr, 1)
                                until(e, s_rhi, b * NHALF + h + 1)
                                e.tensor_tensor(rot[:, 1, :], rot[:, 0, :], rparts[:, 0, cols],
                                                ALU.subtract).then_inc(s_rr1, 1)

                @block.gpsimd
                def _(e):
                    with e.Fori(0, B) as b:
                        for n in range(NQ):
                            t, h = divmod(n, NHALF)
                            cols = slice(h * HALF, (h + 1) * HALF)
                            until(e, s_r1, b * NQ + n + 1)
                            passed(e)
                            e.tensor_copy(parts[:, t, 1, cols], resid[:, n % 2, :]).then_inc(s_mid, 1)
                            until(e, s_mid, b * NQ + n + 1)
                            e.tensor_tensor(parts[:, t, 2, cols], resid[:, n % 2, :], parts[:, t, 1, cols],
                                            ALU.subtract).then_inc(s_lo, 1)
                        if latent:
                            for h in range(NHALF):
                                cols = slice(h * HALF, (h + 1) * HALF)
                                until(e, s_rr1, b * NHALF + h + 1)
                                passed(e)
                                e.tensor_copy(rparts[:, 1, cols], rot[:, 1, :]).then_inc(s_rmid, 1)
                                until(e, s_rmid, b * NHALF + h + 1)
                                e.tensor_tensor(rparts[:, 2, cols], rot[:, 1, :], rparts[:, 1, cols],
                                                ALU.subtract).then_inc(s_rlo, 1)

                @block.sync
                def _(e):
                    prime(e)
                    with e.Fori(0, B) as b:
                        for t in range(2):
                            until(e, s_lo, b * NQ + (t + 1) * NHALF)
                            e.dma_start(qk_dram[t, :, bass.ds(b, 1), :, :].rearrange("n o p t -> p (o n) t"),
                                        parts[:, t, :, :]).then_inc(s_out, 16)
                        if latent:
                            until(e, s_rlo, b * NHALF + NHALF)
                            e.dma_start(rope_dram[:, bass.ds(b, 1), :, :].rearrange("n o p t -> p (o n) t"),
                                        rparts[:, :, :]).then_inc(s_out, 16)
                    until(e, s_out, B * 16 * dma_per_b)
            give_back()

        def attend(causal):
            scale = float((HD + (DR if causal else 0)) ** -0.5)
            stiles = [(j, qc) for j in range(GH) for qc in range(NC)]
            NS = len(stiles)
            ttiles = [(J, kc, j, max(0, (kc - J * CPH) * P) if causal else 0) for J in range(NHALF)
                      for kc in range(min(NC, (J + 1) * CPH) if causal else NC) for j in range(GH)]
            NT = len(ttiles)
            s_max_in, s_exp_in, s_row = ([sem(f"{n}{par}") for par in range(2)]
                                         for n in ("max_stack", "exp_stack", "max_rows"))
            s_s, s_sf = sem("score_tile"), sem("score_max")
            s_mt, s_m = sem("max_turned"), sem("max_split")
            s_mch = sem("split_chain")
            s_st, s_p, s_pv = sem("t_tile"), sem("p_tile"), sem("pv")
            s_o, s_oev, s_ot, s_y, s_ych = sem("o"), sem("o_ev"), sem("o_turned"), sem("y"), sem("y_chain")
            s_vs, s_z = sem("v_stage"), sem("stack_init")
            pair_dmas = len(PAIRS) * 2
            n_exp = pair_dmas + (2 * (len(ROPE_TILE) + len(ROPE_REST) * GH) if causal else 0)
            n_max = 2 * NMAXP * (1 + (GH if causal else 0))
            buf, give_back = of_phase()
            q_exp = [buf(f"q_exp{i}", [P, GH, T], BF16) for i in range(2)]
            k_exp = [buf(f"k_exp{i}", [P, GH, T], BF16) for i in range(2)]
            q_max = [buf(f"q_max{i}", [P, GH, T], BF16) for i in range(2)]
            k_max = [buf(f"k_max{i}", [P, GH, T], BF16) for i in range(2)]
            q_rope = [buf(f"q_rope{i}", [P, T], BF16) for i in range(2)]
            k_rope = [buf(f"k_rope{i}", [P, T], BF16) for i in range(2)]
            vst = [buf(f"vst{i}", [P, NC, GH, 32]) for i in range(2)]
            NPB = 4
            pT = buf("pT", [P, NPB, HALF])
            mx = [buf(f"mx{i}", [P, GH * NC]) for i in range(2)]
            nmr = buf("nmr", [GH * NC, P])
            nmp = [buf(f"nmp{i}", [GH * NC, 3, P], BF16) for i in range(2)]
            o_sb = buf("o_sb", [P, HALF])
            rsum = buf("rsum", [P, CPH, GH, 1])
            NZ = 2 * 4 + 2 * 2 * 2
            s_vz = sem("v_init")

            def qk_rows(t, part, s):
                flat = qk_dram[t, part].rearrange("b (g j d) t -> (b g) d j t", g=NG, j=GH)
                return flat[bass.ds(s, 1)].rearrange("o d j t -> (o d) j t")

            def rope_rows(t, part, s):
                return rope_dram[part, bass.ds(s // NG, 1), t * DR:(t + 1) * DR, :].rearrange("o r t -> (o r) t")

            def load_max(e, s, par):
                for t, dst in ((0, q_max[par]), (1, k_max[par])):
                    for n, pair in enumerate(PAIRS[:NMAXP]):
                        e.dma_start(dst[NROW + n * HD:NROW + (n + 1) * HD, :, :],
                                    qk_rows(t, pair[t], s)).then_inc(s_max_in[par], 16)
                        if causal:
                            for j in range(GH):
                                e.dma_start(dst[n * DR:(n + 1) * DR, j, :],
                                            rope_rows(t, pair[t], s)).then_inc(s_max_in[par], 16)

            def load_exp(e, s, par):
                for t, dst, rope in ((0, q_exp[par], q_rope[par]), (1, k_exp[par], k_rope[par])):
                    for n, pair in enumerate(PAIRS):
                        e.dma_start(dst[n * HD:(n + 1) * HD, :, :], qk_rows(t, pair[t], s)).then_inc(s_exp_in[par], 16)
                    if causal:
                        for n, pair in enumerate(ROPE_TILE):
                            e.dma_start(rope[n * DR:(n + 1) * DR, :], rope_rows(t, pair[t], s)).then_inc(s_exp_in[par], 16)
                        for n, pair in enumerate(ROPE_REST):
                            for j in range(GH):
                                e.dma_start(dst[RROW + n * DR:RROW + (n + 1) * DR, j, :],
                                            rope_rows(t, pair[t], s)).then_inc(s_exp_in[par], 16)

            def events(first, with_s, with_mx):
                ev, k = [], 0
                for u in range(NT):
                    if with_s:
                        while k < NS and k * NT < (u + 1) * NS:
                            ev.append(("S", k))
                            k += 1
                    ev.append(("T", u))
                    if u == first + 1 or u == NT - 1:
                        ev.append(("OE", 0 if u == first + 1 else 1))
                    if with_mx and u == 3:
                        ev.append(("MX", 0))
                    if u == first + 5 or u == NT - 1:
                        ev.append(("OT", 0 if u == first + 5 else 1))
                return ev

            first = [n for n, t in enumerate(ttiles) if t[0] == 0][-1]

            def steps(e, prologue, body):
                prologue(0, 0)
                prologue(1, 1)
                with e.Fori(0, STEPS // 2 - 1) as pair:
                    s = pair * 2
                    body(s, 0, True, True)
                    body(s + 1, 1, True, True)
                body(STEPS - 2, 0, False, True)
                body(STEPS - 1, 1, False, False)

            with nc.Block() as block:
                @block.tensor
                def _(e):
                    until(e, s_z, NZ)

                    def score(s, par, k):
                        j, qc = stiles[k]
                        if k == 0:
                            until(e, s_max_in[par], (s // 2 + 1) * 16 * n_max)
                        if isinstance(s, int) and s * NS + k < 2:
                            pass
                        else:
                            until(e, s_sf, s * NS + k - 1)
                        n = (qc + 1) * P if causal else T
                        for h in range((n + HALF - 1) // HALF):
                            w = min(HALF, n - h * HALF)
                            diag = causal and h * HALF + w == n
                            ins = e.matmul(wide[k % 2][:, h * HALF:h * HALF + w],
                                           q_max[par][0:KMAX, j, qc * P:(qc + 1) * P],
                                           k_max[par][0:KMAX, j, h * HALF:h * HALF + w], start=True, stop=not diag)
                            if diag:
                                ins = e.matmul(wide[k % 2][:, n - P:n], identb[:, :], mask_qk[:, :],
                                               start=False, stop=True)
                        ins.then_inc(s_s, 1)

                    def t_score(s, par, u):
                        J, kc, j, q0 = ttiles[u]
                        if u == 0:
                            until(e, s_exp_in[par], (s // 2 + 1) * 16 * n_exp)
                            until(e, s_row[par], (s // 2 + 1) * 48)
                        if isinstance(s, int) and s * NT + u < 2:
                            pass
                        else:
                            until(e, s_p, s * NT + u - 1)
                        dst = bank[u % 2][:, q0:HALF]
                        keys = slice(kc * P, (kc + 1) * P)
                        qs = slice(J * HALF + q0, (J + 1) * HALF)
                        if causal:
                            e.matmul(dst, k_rope[par][:, keys], q_rope[par][:, qs], start=True, stop=False)
                        diag = causal and kc >= J * CPH
                        ins = e.matmul(dst, k_exp[par][:, j, keys], q_exp[par][:, j, qs], start=not causal, stop=not diag)
                        if diag:
                            ins = e.matmul(bank[u % 2][:, q0:q0 + P], identb[:, :], mask_kq[:, :],
                                           start=False, stop=True)
                        ins.then_inc(s_st, 1)

                    def weigh(s, par, u):
                        J, kc, j, q0 = ttiles[u]
                        if u == 0:
                            until(e, s_vz, 4)
                            until(e, s_vs, s + 1)
                        if u in (0, first + 1):
                            until(e, s_oev, s * NHALF + J)
                        until(e, s_p, s * NT + u + 1)
                        last = kc == (min(NC, (J + 1) * CPH) if causal else NC) - 1
                        ins = e.matmul(bank[2][32 * j:32 * (j + 1), q0:HALF], vst[par][:, kc, j, :],
                                       pT[:, u % NPB, q0:HALF], start=(kc == 0), stop=last,
                                       tile_position=(0, 32 * j), skip_group_check=True)
                        ins.then_inc(s_pv, 1)

                    def turn_max(s, par):
                        until(e, s_sf, (s + 1) * NS)
                        until(e, s_y, s * NHALF if isinstance(s, int) and s < 1 else (s - 1) * NHALF)
                        e.transpose(bank[3][0:GH * NC, 0:P], mx[par][:, :], ident[:, :]).then_inc(s_mt, 1)

                    def turn_out(s, J):
                        until(e, s_oev, s * NHALF + J + 1)
                        until(e, s_y, s * NHALF + J)
                        until(e, s_m, s + 1 + (1 if not (isinstance(s, int) and s == STEPS - 1) else 0))
                        for c in range(CPH):
                            ins = e.transpose(bank[3][:, c * P:(c + 1) * P], o_sb[:, c * P:(c + 1) * P], ident[:, :])
                        ins.then_inc(s_ot, 1)

                    def prologue(s, par):
                        for k in range(NS):
                            score(s, par, k)
                        if s == 0:
                            turn_max(0, 0)

                    def body(s, par, with_s, with_mx):
                        t_score(s, par, 0)
                        t_score(s, par, 1)
                        for what, n in events(first, with_s, with_mx):
                            if what == "S":
                                score(s + 2, par, n)
                            elif what == "T":
                                weigh(s, par, n)
                                if n + 2 < NT:
                                    t_score(s, par, n + 2)
                            elif what == "MX":
                                turn_max(s + 1, 1 - par)
                            elif what == "OT":
                                turn_out(s, n)

                    steps(e, prologue, body)

                @block.vector
                def _(e):
                    for par in range(2):
                        e.memset(q_exp[par][32:64, :, :], 0.0).then_inc(s_z, 1)
                        e.memset(k_exp[par][32:64, :, :], 1.0).then_inc(s_z, 1)
                        e.memset(q_exp[par][64:128, :, :], 0.0).then_inc(s_z, 1)
                        e.memset(k_exp[par][64:128, :, :], 0.0).then_inc(s_z, 1)
                        for m in (q_max[par], k_max[par]):
                            for r in (0, 64):
                                w = 64 if r == 0 else 32
                                e.memset(m[r:r + w, :, :], 0.0).then_inc(s_z, 1)

                    def score(s, par, k):
                        j, qc = stiles[k]
                        n = (qc + 1) * P if causal else T
                        until(e, s_s, s * NS + k + 1)
                        if k == 0 and not (isinstance(s, int) and s < 2):
                            until(e, s_mt, s - 1)
                        e.tensor_reduce(mx[par][:, j * NC + qc:j * NC + qc + 1], wide[k % 2][:, 0:n], AX.X,
                                        ALU.max).then_inc(s_sf, 1)

                    def split_max(s, par):
                        until(e, s_mt, s + 1)
                        if not (isinstance(s, int) and s < 2):
                            until(e, s_row[par], s // 2 * 48)
                        src = bank[3][0:GH * NC, 0:P]
                        e.tensor_scalar(nmp[par][:, 0, :], src, -1.0, None, ALU.mult).then_inc(s_mch, 1)
                        until(e, s_mch, s * 3 + 1)
                        e.scalar_tensor_tensor(nmr[:, :], src, -1.0, nmp[par][:, 0, :], ALU.mult,
                                               ALU.subtract).then_inc(s_mch, 1)
                        until(e, s_mch, s * 3 + 2)
                        e.tensor_copy(nmp[par][:, 1, :], nmr[:, :]).then_inc(s_mch, 1)
                        until(e, s_mch, s * 3 + 3)
                        e.tensor_tensor(nmp[par][:, 2, :], nmr[:, :], nmp[par][:, 1, :], ALU.subtract).then_inc(s_m, 1)

                    def normalize(s, J):
                        until(e, s_ot, s * NHALF + J + 1)
                        o = bank[3][:, :].rearrange("p (c j r) -> p c j r", c=CPH, j=GH)
                        e.reciprocal(rsum[:, :, :, :], o[:, :, :, HD:HD + 1]).then_inc(s_ych, 1)
                        until(e, s_ych, s * NHALF + J + 1)
                        dst = y_all.rearrange("p b g c d -> p (b g) c d")[:, bass.ds(s, 1), J * CPH:(J + 1) * CPH, :]
                        e.tensor_tensor(dst.rearrange("p o c (j d) -> p (o c) j d", j=GH), o[:, :, :, 0:HD],
                                        rsum[:, :, :, :].broadcast_to([P, CPH, GH, HD]), ALU.mult).then_inc(s_y, 1)

                    def prologue(s, par):
                        for k in range(NS):
                            score(s, par, k)
                        if s == 0:
                            split_max(0, 0)

                    def body(s, par, with_s, with_mx):
                        for what, n in events(first, with_s, with_mx):
                            if what == "S":
                                score(s + 2, par, n)
                            elif what == "MX":
                                split_max(s + 1, 1 - par)
                            elif what == "OT":
                                normalize(s, n)

                    steps(e, prologue, body)

                @block.scalar
                def _(e):
                    def body(s, par, with_s, with_mx):
                        for what, n in events(first, with_s, with_mx):
                            if what == "T":
                                q0 = ttiles[n][3]
                                until(e, s_st, s * NT + n + 1)
                                if not (isinstance(s, int) and s * NT + n < NPB):
                                    until(e, s_pv, s * NT + n + 1 - NPB if n + 1 > NPB else (s * NT + n + 1 - NPB))
                                e.activation(pT[:, n % NPB, q0:HALF], bank[n % 2][:, q0:HALF], ACT.Exp,
                                             scale=scale).then_inc(s_p, 1)
                            elif what == "OE":
                                end = first + 1 if n == 0 else NT
                                until(e, s_pv, s * NT + end)
                                if not (isinstance(s, int) and s * NHALF + n == 0):
                                    until(e, s_ot, s * NHALF + n)
                                e.activation(o_sb[:, :], bank[2][:, :], ACT.Copy).then_inc(s_oev, 1)

                    body(0, 0, True, True)
                    body(1, 1, True, True)
                    with e.Fori(1, STEPS // 2 - 1) as pair:
                        s = pair * 2
                        body(s, 0, True, True)
                        body(s + 1, 1, True, True)
                    body(STEPS - 2, 0, False, True)
                    body(STEPS - 1, 1, False, False)

                @block.gpsimd
                def _(e):
                    def stage_v(s, par):
                        src = v_all.rearrange("p b g c d -> p (b g) c d")[:, bass.ds(s, 1), :, :]
                        e.tensor_copy(vst[par][:, :, :, 0:HD],
                                      src.rearrange("p o c (j d) -> p (o c) j d", j=GH)).then_inc(s_vs, 1)

                    for v in vst:
                        e.memset(v[:, :, :, :], 0.0).then_inc(s_vz, 1)
                    until(e, s_vz, 2)
                    for v in vst:
                        e.memset(v[:, :, :, HD:HD + 1], 1.0).then_inc(s_vz, 1)
                    stage_v(0, 0)
                    stage_v(1, 1)
                    with e.Fori(0, STEPS // 2 - 1) as pair:
                        s = pair * 2
                        for par in range(2):
                            until(e, s_pv, (s + par + 1) * NT)
                            passed(e)
                            stage_v(s + par + 2, par)

                @block.sync
                def _(e):
                    prime(e)
                    def rows(s, par):
                        until(e, s_m, s + 1)
                        for i in range(3):
                            dst = q_exp[par][MROW + i:MROW + i + 1, :, :].rearrange("o j (c q) -> o (j c) q", q=P)
                            e.dma_start(dst, nmp[par][:, i, :]).then_inc(s_row[par], 16)

                    until(e, s_z, NZ)
                    load_max(e, 0, 0)
                    load_exp(e, 0, 0)
                    load_max(e, 1, 1)
                    load_exp(e, 1, 1)
                    rows(0, 0)
                    with e.Fori(0, STEPS // 2 - 1) as pair:
                        s = pair * 2
                        for par in range(2):
                            until(e, s_sf, (s + par + 1) * NS)
                            load_max(e, s + par + 2, par)
                            rows(s + par + 1, 1 - par)
                            until(e, s_st, (s + par + 1) * NT)
                            load_exp(e, s + par + 2, par)
                    rows(STEPS - 1, 1)
                    for par in range(2):
                        until(e, s_row[par], STEPS // 2 * 48)
            give_back()

        def add_projected():
            buf, give_back = of_phase()
            stage = buf("stage", [P, NC, D])
            stT = buf("stT", [P, T])
            s_g, s_t, s_tev, s_mm, s_add = sem("gathered"), sem("turned"), sem("turned_ev"), sem("o_proj"), sem("added")
            with nc.Block() as block:
                @block.sync
                def _(e):
                    prime(e)

                @block.gpsimd
                def _(e):
                    with e.Fori(0, B) as b:
                        until(e, s_t, b * NHALF)
                        passed(e)
                        for g in range(NG):
                            src = y_all[:, bass.ds(b, 1), g, :, :].rearrange("p o c d -> p (o c) d")
                            ins = e.tensor_copy(stage[:, :, g * 32:(g + 1) * 32], src)
                        ins.then_inc(s_g, 1)

                @block.tensor
                def _(e):
                    with e.Fori(0, B) as b:
                        until(e, s_g, b + 1)
                        for h in range(NHALF):
                            for c in range(CPH):
                                ins = e.transpose(bank[h][:, c * P:(c + 1) * P], stage[:, h * CPH + c, :], ident[:, :])
                            ins.then_inc(s_t, 1)
                        until(e, s_add, b * NHALF)
                        for h in range(NHALF):
                            until(e, s_tev, b * NHALF + h + 1)
                            for c in range(CPH):
                                at = h * CPH + c
                                ins = e.matmul(bank[2 + h][:, c * P:(c + 1) * P], stT[:, at * P:(at + 1) * P],
                                               wa[:, 4, :], start=True, stop=True)
                            ins.then_inc(s_mm, 1)

                @block.scalar
                def _(e):
                    with e.Fori(0, B) as b:
                        until(e, s_mm, b * NHALF)
                        for h in range(NHALF):
                            until(e, s_t, b * NHALF + h + 1)
                            e.activation(stT[:, h * HALF:(h + 1) * HALF], bank[h][:, :], ACT.Copy).then_inc(s_tev, 1)

                @block.vector
                def _(e):
                    with e.Fori(0, B) as b:
                        for h in range(NHALF):
                            until(e, s_mm, b * NHALF + h + 1)
                            rows = x_sb[:, bass.ds(b * NC + h * CPH, CPH), :]
                            e.tensor_tensor(rows, bank[2 + h][:, :].rearrange("p (c d) -> p c d", c=CPH), rows,
                                            ALU.add).then_inc(s_add, 1)
            give_back()

        def add_plain():
            with nc.Block() as block:
                @block.vector
                def _(e):
                    with e.Fori(0, B) as b:
                        for g in range(NG):
                            rows = x_sb[:, bass.ds(b * NC, NC), g * 32:(g + 1) * 32]
                            y = y_all[:, bass.ds(b, 1), g, :, :].rearrange("p o c d -> p (o c) d")
                            e.tensor_tensor(rows, rows, y, ALU.add)

        def route():
            buf, give_back = of_phase()
            ln = Norm(buf)
            xnT = ln.buffers[1]
            s_lg, s_lev, s_cp = sem("logits"), sem("logits_ev"), sem("xnT_kept")
            with nc.Block() as block:
                @block.sync
                def _(e):
                    prime(e)

                @block.tensor
                def _(e):
                    with e.Fori(0, B) as b:
                        ln.tensor(e, b)
                        until(e, ln.ev, b * NHALF + NHALF)
                        until(e, s_lev, b)
                        for c in range(NC):
                            ins = e.matmul(bank[2][:, c * NE:(c + 1) * NE], xnT[:, c * P:(c + 1) * P], rwt[:, :],
                                           start=True, stop=True)
                        ins.then_inc(s_lg, 1)

                @block.scalar
                def _(e):
                    with e.Fori(0, B) as b:
                        ln.scalar_std(e, b)
                        until(e, s_cp, b)
                        ln.scalar_evac(e, b, s_lg, b)

                @block.gpsimd
                def _(e):
                    with e.Fori(0, B) as b:
                        until(e, ln.ev, b * NHALF + NHALF)
                        passed(e)
                        e.tensor_copy(xnT_all[:, bass.ds(b, 1), :].rearrange("p o t -> p (o t)"),
                                      xnT[:, :]).then_inc(s_cp, 1)

                @block.vector
                def _(e):
                    with e.Fori(0, B) as b:
                        ln.vector(e, b)
                        until(e, s_lg, b + 1)
                        e.tensor_copy(sc[:, :, bass.ds(b, 1), :].rearrange("p c o e -> p (c o) e"),
                                      bank[2][:, 0:NC * NE].rearrange("p (c e) -> p c e", c=NC)).then_inc(s_lev, 1)
            give_back()

        def choose():
            buf, give_back = of_phase()
            scm = buf("scm", [P, NC, B])
            work = buf("work", [B * NE, T])
            cand = buf("cand", [B * NE, T])
            top8 = buf("top8", [B * NE, 8])
            topc = buf("topc", [B * NE, 1])
            s_v, s_a, s_t, s_g = sem("choose_v"), sem("choose_exp"), sem("scores_turned"), sem("gates_turned")
            s_gt = sem("gates_back")
            with nc.Block() as block:
                @block.sync
                def _(e):
                    prime(e)

                @block.vector
                def _(e):
                    n = [0]

                    def then(ins):
                        n[0] += 1
                        ins.then_inc(s_v, 1)
                        until(e, s_v, n[0])

                    rows = sc.rearrange("p c b e -> p (c b) e")
                    m = scm.rearrange("p c b -> p (c b)")
                    mb = scm.rearrange("p c (b o) -> p (c b) o", o=1).broadcast_to([P, NC * B, NE])
                    then(e.tensor_reduce(m, rows, AX.X, ALU.max))
                    then(e.tensor_tensor(rows, rows, mb, ALU.subtract))
                    until(e, s_a, 1)
                    then(e.tensor_reduce(m, rows, AX.X, ALU.add))
                    then(e.reciprocal(m, m))
                    then(e.tensor_tensor(rows, rows, mb, ALU.mult))
                    until(e, s_t, 1)
                    e.tensor_copy(scT[:, :], wide[0][0:B * NE, :])
                    then(e.tensor_copy(work[:, :], wide[0][0:B * NE, :]))
                    base = n[0]
                    with e.Fori(0, ROUNDS) as r:
                        e.max(top8[:, :], work[:, :]).then_inc(s_v, 1)
                        until(e, s_v, r * 2 + base + 1)
                        passed(e)
                        e.match_replace(work[:, :], top8[:, :], work[:, :], -1.0).then_inc(s_v, 1)
                        until(e, s_v, r * 2 + base + 2)
                    n[0] += 2 * ROUNDS
                    then(e.max(top8[:, :], work[:, :]))
                    then(e.scalar_tensor_tensor(cand[:, :], work[:, :], top8[:, 0:1], rev[:, :], ALU.is_equal, ALU.mult))
                    then(e.tensor_reduce(topc[:, :], cand[:, :], AX.X, ALU.max))
                    then(e.tensor_scalar(cand[:, :], cand[:, :], topc[:, 0:1], None, ALU.is_equal))
                    then(e.scalar_tensor_tensor(cand[:, :], work[:, :], 0.0, cand[:, :], ALU.is_lt, ALU.add))
                    e.tensor_tensor(scT[:, :], scT[:, :], cand[:, :], ALU.mult).then_inc(s_g, 1)
                    until(e, s_gt, 1)
                    e.tensor_copy(gate[:, :, :], bank[0][:, 0:NC * B * NE].rearrange("p (c r) -> p c r", c=NC))

                @block.scalar
                def _(e):
                    rows = sc.rearrange("p c b e -> p (c b e)")
                    until(e, s_v, 2)
                    e.activation(rows, rows, ACT.Exp).then_inc(s_a, 1)

                @block.tensor
                def _(e):
                    until(e, s_v, 5)
                    for c in range(NC):
                        ins = e.transpose(wide[0][0:B * NE, c * P:(c + 1) * P],
                                          sc[:, c, :, :].rearrange("p b e -> p (b e)"), ident[:, :])
                    ins.then_inc(s_t, 1)
                    until(e, s_g, 1)
                    for c in range(NC):
                        ins = e.transpose(bank[0][:, c * B * NE:(c + 1) * B * NE], scT[:, c * P:(c + 1) * P],
                                          ident[0:B * NE, 0:B * NE])
                    ins.then_inc(s_gt, 1)
            give_back()

        def experts():
            buf, give_back = of_phase()
            hT = buf("hT", [P, 2, KH, HALF])
            s_h, s_a, s_y, s_add = sem("hidden"), sem("gelu"), sem("expert_out"), sem("added")
            s_b, s_bx = sem("bias"), sem("bias_added")
            units = [(ex, J) for ex in range(NE) for J in range(NHALF)]
            NU = len(units)
            hb = [bank[0], bank[1], wide[0][:, 0:HALF], wide[0][:, HALF:2 * HALF]]
            yb = [bank[2], bank[3]]
            with nc.Block() as block:
                @block.sync
                def _(e):
                    prime(e)

                @block.tensor
                def _(e):
                    def hidden(b, u):
                        ex, J = units[u]
                        for k in range(KH):
                            until(e, s_a, b * NU * KH + u * KH + k + 1)
                            e.matmul(hb[k][:, :], w1_sb[:, ex, k * P:(k + 1) * P],
                                     xnT_all[:, bass.ds(b, 1), J * HALF:(J + 1) * HALF].rearrange("p o t -> p (o t)"),
                                     start=True, stop=True).then_inc(s_h, 1)

                    def back(b, u):
                        ex, J = units[u]
                        until(e, s_a, b * NU * KH + (u + 2) * KH)
                        if u >= 2:
                            until(e, s_add, b * NU + u - 1)
                        else:
                            until(e, s_add, b * NU)
                        for c in range(CPH):
                            for k in range(KH):
                                ins = e.matmul(yb[u % 2][:, c * P:(c + 1) * P], hT[:, u % 2, k, c * P:(c + 1) * P],
                                               w2_sb[:, ex, k, :], start=(k == 0), stop=(k == KH - 1))
                        ins.then_inc(s_y, 1)

                    for b in range(B):
                        for h in range(NHALF):
                            until(e, s_bx, max(0, b * NHALF + h - 1))
                            for c in range(CPH):
                                at = h * CPH + c
                                ins = e.matmul(wide[1][:, h * HALF + c * D:h * HALF + (c + 1) * D],
                                               scT[:, at * P:(at + 1) * P], b2blk[:, b, :], start=True, stop=True)
                            ins.then_inc(s_b, 1)
                    until(e, s_bx, B * NHALF)
                    with e.Fori(0, B) as b:
                        hidden(b, 0)
                        for u in range(NU):
                            if u + 1 < NU:
                                hidden(b, u + 1)
                            back(b, u)

                @block.scalar
                def _(e):
                    e.drain().then_inc(s_a, KH)
                    with e.Fori(0, B) as b:
                        for u in range(NU):
                            ex, J = units[u]
                            if u >= 2:
                                until(e, s_y, b * NU + u - 1)
                            else:
                                until(e, s_y, b * NU)
                            for k in range(KH):
                                until(e, s_h, b * NU * KH + u * KH + k + 1)
                                e.activation(hT[:, u % 2, k, :], hb[k][:, :], ACT.Gelu,
                                             bias=b1t[:, ex * KH + k:ex * KH + k + 1]).then_inc(s_a, 1)

                @block.vector
                def _(e):
                    for b in range(B):
                        for h in range(NHALF):
                            until(e, s_b, b * NHALF + h + 1)
                            rows = x_sb[:, b * NC + h * CPH:b * NC + (h + 1) * CPH, :]
                            e.tensor_tensor(rows, wide[1][:, h * HALF:(h + 1) * HALF].rearrange("p (c d) -> p c d", c=CPH),
                                            rows, ALU.add).then_inc(s_bx, 1)
                    until(e, s_bx, B * NHALF)
                    with e.Fori(0, B) as b:
                        for u in range(NU):
                            ex, J = units[u]
                            until(e, s_y, b * NU + u + 1)
                            if u >= 1:
                                until(e, s_add, b * NU + u)
                            else:
                                until(e, s_add, b * NU)
                            for c in range(CPH):
                                at = J * CPH + c
                                row = x_sb[:, bass.ds(b * NC + at, 1), :].rearrange("p o d -> p (o d)")
                                ins = e.scalar_tensor_tensor(
                                    row, yb[u % 2][:, c * P:(c + 1) * P],
                                    gate[:, at, bass.ds(b * NE + ex, 1)], row, ALU.mult, ALU.add)
                            ins.then_inc(s_add, 1)
            give_back()

        def store():
            s_st = sem("stored")
            with nc.Block() as block:
                @block.sync
                def _(e):
                    prime(e)
                    e.dma_start(out.rearrange("b (c p) d -> p (b c) d", p=P), x_sb[:, :, :]).then_inc(s_st, 16)
                    until(e, s_st, 16)

        load()
        project(True)
        attend(True)
        add_projected()
        route()
        choose()
        experts()
        project(False)
        attend(False)
        add_plain()
        route()
        choose()
        experts()
        store()


_INS = ["L0_attn_a_x", "L0_attn_a_W_kv_down", "L0_attn_a_W_k_up", "L0_attn_a_W_v_up", "L0_attn_a_W_q",
        "L0_attn_a_W_q_rope", "L0_attn_a_W_k_rope", "L0_attn_a_W_o", "L0_attn_b_Wq", "L0_attn_b_Wk",
        "L0_attn_b_Wv", "L0_ffn_router_w", "L0_ffn_w1", "L0_ffn_b1", "L0_ffn_w2", "L0_ffn_b2"]


def rope_tables():
    import numpy as np
    inv = (1.0 / 10000.0 ** (np.arange(0, DR, 2, dtype=np.float32) / np.float32(DR))).astype(np.float32)
    ang = np.outer(inv, np.arange(T, dtype=np.float32)).astype(np.float32)
    c, s = np.cos(ang).astype(np.float32), np.sin(ang).astype(np.float32)
    return np.concatenate([c, c], 0), np.concatenate([-s, s], 0)


def kernel(**inputs):
    import numpy as np
    import concourse.bacc as bacc
    from concourse.bass_utils import run_bass_kernel_spmd as run

    nc = bacc.Bacc("TRN2", target_bir_lowering=False, num_devices=1)
    arrays, args = {}, []
    named = [(n, np.ascontiguousarray(inputs[n])) for n in _INS]
    named += list(zip(("rope_cos", "rope_sin"), rope_tables()))
    for name, a in named:
        arrays[f"in_{name}"] = a
        args.append(nc.dram_tensor(f"in_{name}", a.shape, mybir.dt.from_np(a.dtype), kind="ExternalInput").ap())
    args.append(nc.dram_tensor("out_0", (B, T, D), F32, kind="ExternalOutput").ap())
    mk_program(nc, *args)
    r = run(nc, [arrays], core_ids=[0])
    return r.results[0]["out_0"]
```

```python
from contextlib import ExitStack

import concourse.bass as bass
from concourse import mybir

F32 = mybir.dt.float32
BF16 = mybir.dt.bfloat16
I32, U32 = mybir.dt.int32, mybir.dt.uint32
ALU = mybir.AluOpType
ACT = mybir.ActivationFunctionType
AX = mybir.AxisListType

P = 128
B, T, D = 4, 1024, 128
NC = T // P
HALF = 512
NHALF = T // HALF
CPH = HALF // P
HD = 8
GH = 4
NG = D // HD // GH
STEPS = B * NG
DR = 32
NE, HID = 8, 512
KH = HID // P
CAP = max(1, int(T * 2.0 / NE) + 1)
ROUNDS, REST = divmod(CAP, 8)
assert REST == 1 and CAP == 2 * P + 1
NFACT = 5
NM = B * 2
EPS = 1e-5
BIG = -1e30
PRIME = 2

PAIRS = [(0, 0), (0, 1), (0, 2), (1, 0), (1, 1), (2, 0)]
MAX_PAIRS = [(0, 0), (0, 1), (1, 0)]
NMAXP = len(MAX_PAIRS)
ROPE_TILE = [(0, 0), (0, 1), (1, 0), (1, 1)]
ROPE_REST = [(0, 2), (2, 0)]
MROW = len(PAIRS) * HD
RROW = 64
NROW = NMAXP * DR
KMAX = NROW + NMAXP * HD


def mk_program(nc, x_in, w_kv_down, w_k_up, w_v_up, w_q, w_q_rope, w_k_rope, w_o, wq_b, wk_b, wv_b,
               router_w, w1, b1, w2, b2, cos2, sin2, out):
    ctx = ExitStack()
    with ctx:
        def sb(name, shape, dt=F32):
            return ctx.enter_context(nc.sbuf_tensor(name, shape, dt))

        def pb(name, dt=F32):
            return ctx.enter_context(nc.psum_tensor(name, [P, 2 * HALF if name.endswith("_2") else HALF], dt))

        names, fresh, bare = [0], [], []
        over, ended, spare_sems = [], [], []

        def sem(name, primed=True):
            names[0] += 1
            if primed and spare_sems:
                made = spare_sems.pop()
            else:
                made = ctx.enter_context(nc.semaphore(f"{name}_{names[0]}"))
            (fresh if primed else bare).append(made)
            return made

        def prime(e):
            for made in over:
                e.sem_clear(made)
            for made in fresh:
                e.sem_inc(made, PRIME)
            spare_sems.extend(ended)
            ended[:] = over
            over[:] = fresh
            fresh.clear()

        def until(e, semaphore, count):
            e.wait_ge(semaphore, count + (0 if any(semaphore is one for one in bare) else PRIME))

        s_passed = sem("passed", False)

        def passed(e):
            e.sem_inc(s_passed, 1)

        x_sb = sb("x_sb", [P, B * NC, D])
        ident = sb("ident", [P, P])
        identb = sb("identb", [P, P], BF16)
        mask_qk = sb("mask_qk", [P, P], BF16)
        mask_kq = sb("mask_kq", [P, P], BF16)
        wa = sb("wa", [P, 5, D])
        wqk = sb("wqk", [P, 2, D])
        wr = sb("wr", [P, 4, DR])
        wbn = sb("wbn", [P, 3, D])
        wbt = sb("wbt", [P, 3, D])
        cs = sb("cs", [2 * DR, 2, T])
        b1n = sb("b1n", [NE * KH, P])
        b1t = sb("b1t", [P, NE * KH])
        b2blk = sb("b2blk", [B * NE, B, D])
        rwn = sb("rwn", [NE, D])
        rwt = sb("rwt", [P, NE])
        rev = sb("rev", [B * NE, T])
        v_all = sb("v_all", [P, B, NG, NC, GH * HD])
        y_all = sb("y_all", [P, B, NG, NC, GH * HD])
        sc = sb("sc", [P, NC, B, NE])
        facts = sb("facts", [P, NC, B * NE, NFACT], BF16)
        slot_of = sb("slot_of", [P, NC, B * NE])
        slots = sb("slots", [P, 2 * P], BF16)
        own = sb("own", [B * NE, NE])
        spare = sb("spare", [B * NE, 1])
        first_row = sb("first_row", [B * NE, 1])
        ints = sb("ints", [B * NE, NE + 1], I32)
        last_tok = sb("last_tok", [B * NE, 1], U32)
        last_to = sb("last_to", [B * NE, NE])
        last_gate = sb("last_gate", [B * NE, 1])
        scT = sb("scT", [B * NE, T])

        def of_phase():
            own = ExitStack()
            names[0] += 1
            tag = names[0]
            return (lambda name, shape, dt=F32: own.enter_context(nc.sbuf_tensor(f"{name}_{tag}", shape, dt))), own.close

        bank = [pb(f"bank{i}") for i in range(4)]
        wide = [pb(f"wide{i}_2") for i in range(2)]

        qk_dram = nc.dram_tensor("qk_parts", [2, 3, B, P, T], BF16, kind="Internal").ap()
        xn_dram = nc.dram_tensor("xn_rows", [B * T, D], F32, kind="Internal").ap()
        acc_dram = nc.dram_tensor("acc_rows", [B * T + B * NE, D], F32, kind="Internal").ap()
        rope_dram = nc.dram_tensor("rope_parts", [3, B, 2 * DR, T], BF16, kind="Internal").ap()

        def load():
            s_ld, s_b2, s_c, s_t = sem("loaded"), sem("b2_loaded"), sem("consts"), sem("turned")
            s_i = sem("ints")
            loads = [(x_sb[:, :, :], x_in.rearrange("b (c p) d -> p (b c) d", p=P))]
            loads += [(wa[:, n, :], w) for n, w in enumerate((w_q, w_kv_down, w_k_up, w_v_up, w_o))]
            for n, w in ((0, w_q_rope), (2, w_k_rope)):
                h = DR // 2
                loads += [(wr[:, n, :], w), (wr[:, n + 1, 0:h], w[:, h:DR]), (wr[:, n + 1, h:DR], w[:, 0:h])]
            loads += [(wbn[:, n, :], w) for n, w in enumerate((wq_b, wk_b, wv_b))]
            loads += [(cs[n * DR:(n + 1) * DR, i, :], t) for n in range(2) for i, t in enumerate((cos2, sin2))]
            loads += [(b1n[:, :], b1.rearrange("e (k p) -> (e k) p", p=P)), (rwn[:, :], router_w)]
            with nc.Block() as block:
                @block.sync
                def _(e):
                    prime(e)
                    for dst, src in loads:
                        e.dma_start(dst, src).then_inc(s_ld, 16)
                    until(e, s_c, 5)
                    for b in range(B):
                        e.dma_start(b2blk[b * NE:(b + 1) * NE, b, :], b2).then_inc(s_b2, 16)
                    until(e, s_ld, 16 * len(loads))
                    until(e, s_b2, 16 * B)

                @block.gpsimd
                def _(e):
                    for m, v in ((ident, 0.0), (identb, 0.0), (mask_qk, 0.0), (mask_kq, 0.0)):
                        e.memset(m[:, :], v).then_inc(s_c, 1)
                    e.memset(b2blk[:, :, :], 0.0).then_inc(s_c, 1)
                    until(e, s_c, 5)
                    for m in (ident, identb):
                        e.affine_select(out=m[:, :], in_=m[:, :], compare_op=ALU.not_equal, fill=1.0, base=0,
                                        pattern=[[-1, P]], channel_multiplier=1).then_inc(s_c, 1)
                    e.affine_select(out=mask_qk[:, :], in_=mask_qk[:, :], compare_op=ALU.is_ge, fill=BIG, base=0,
                                    pattern=[[-1, P]], channel_multiplier=1).then_inc(s_c, 1)
                    e.affine_select(out=mask_kq[:, :], in_=mask_kq[:, :], compare_op=ALU.is_ge, fill=BIG, base=0,
                                    pattern=[[1, P]], channel_multiplier=-1).then_inc(s_c, 1)
                    e.iota(rev[:, :], pattern=[[-1, T]], base=T, channel_multiplier=0,
                           allow_small_or_imprecise_dtypes=True).then_inc(s_c, 1)
                    e.iota(facts[:, :, :, 0], pattern=[[0, NC], [0, B * NE]], base=0, channel_multiplier=1,
                           allow_small_or_imprecise_dtypes=True)
                    for c in range(NC):
                        e.iota(facts[:, c, :, 1], pattern=[[T, B], [0, NE]], base=c * P, channel_multiplier=0,
                               allow_small_or_imprecise_dtypes=True)
                    e.iota(slots[:, :], pattern=[[1, 2 * P]], base=0, channel_multiplier=0,
                           allow_small_or_imprecise_dtypes=True)
                    e.iota(spare[:, :], pattern=[[0, 1]], base=B * T, channel_multiplier=1,
                           allow_small_or_imprecise_dtypes=True)
                    e.iota(ints[:, 0:NE], pattern=[[-1, NE]], base=NE, channel_multiplier=1)
                    e.iota(ints[:, NE:NE + 1], pattern=[[0, 1]], base=0, channel_multiplier=T // NE).then_inc(s_c, 1)

                @block.tensor
                def _(e):
                    until(e, s_c, 7)
                    until(e, s_ld, 16 * len(loads))
                    for n in range(3):
                        e.transpose(bank[0][:, n * D:(n + 1) * D], wbn[:, n, :], ident[:, :])
                    e.transpose(bank[1][:, 0:NE * KH], b1n[:, :], ident[0:NE * KH, 0:NE * KH])
                    e.transpose(bank[1][:, 64:64 + NE], rwn[:, :], ident[0:NE, 0:NE]).then_inc(s_t, 1)

                @block.vector
                def _(e):
                    until(e, s_t, 1)
                    for n in range(2):
                        e.tensor_copy(dim_major(wbt[:, n, :]), by_dim(bank[0][:, n * D:(n + 1) * D]))
                        e.tensor_copy(dim_major(wqk[:, n, :]), by_dim(wa[:, 2 * n, :]))
                    e.tensor_copy(wbt[:, 2, :], bank[0][:, 2 * D:3 * D])
                    e.tensor_copy(b1t[:, :], bank[1][:, 0:NE * KH])
                    until(e, s_c, 11)
                    e.tensor_scalar(ints[:, 0:NE], ints[:, 0:NE], NE - 1, None, ALU.bitwise_and).then_inc(s_i, 1)
                    e.tensor_scalar(ints[:, NE:NE + 1], ints[:, NE:NE + 1], -T, None, ALU.bitwise_and).then_inc(s_i, 1)
                    until(e, s_i, 2)
                    e.tensor_scalar(own[:, :], ints[:, 0:NE], 0.0, None, ALU.is_equal)
                    e.tensor_copy(first_row[:, :], ints[:, NE:NE + 1])
                    e.tensor_copy(rwt[:, :], bank[1][:, 64:64 + NE])

        def by_dim(ap):
            return ap.rearrange("p (g j d) -> p g d j", g=NG, j=GH)

        def dim_major(ap):
            return ap.rearrange("p (g d j) -> p g d j", g=NG, j=GH)

        class Norm:

            def __init__(self, buf):
                self.buffers = (buf("xn", [P, NC, D]), buf("xnT", [P, T]), buf("stats", [P, NC, 6]),
                                buf("lnv", [P, 5, NC]))
                self.st, self.var, self.std = sem("ln_stat"), sem("ln_var"), sem("ln_std")
                self.xn, self.tr, self.ev = sem("ln_xn"), sem("ln_tr"), sem("ln_ev")
                self.ch = sem("ln_chain")

            def vector(self, e, b):
                xn, xnT, stats, lnv = self.buffers
                for c in range(NC):
                    ins = e.bn_stats(stats[:, c, :], x_sb[:, bass.ds(b * NC + c, 1), :].rearrange("p o d -> p (o d)"))
                ins.then_inc(self.ch, 1)
                me, mo = stats[:, :, 1], stats[:, :, 4]
                until(e, self.ch, b * 6 + 1)
                e.tensor_tensor(lnv[:, 0, :], me, mo, ALU.subtract).then_inc(self.ch, 1)
                e.tensor_tensor(lnv[:, 1, :], stats[:, :, 2], stats[:, :, 5], ALU.add)
                e.tensor_tensor(lnv[:, 2, :], me, mo, ALU.add).then_inc(self.ch, 1)
                until(e, self.ch, b * 6 + 3)
                e.scalar_tensor_tensor(lnv[:, 3, :], lnv[:, 0, :], 0.25, lnv[:, 0, :],
                                       ALU.mult, ALU.mult).then_inc(self.ch, 1)
                e.tensor_scalar(lnv[:, 1, :], lnv[:, 1, :], 1.0 / D, EPS, ALU.mult, ALU.add)
                e.tensor_scalar(lnv[:, 2, :], lnv[:, 2, :], 0.5, None, ALU.mult).then_inc(self.ch, 1)
                until(e, self.ch, b * 6 + 5)
                e.tensor_tensor(lnv[:, 3, :], lnv[:, 1, :], lnv[:, 3, :], ALU.add).then_inc(self.var, 1)
                until(e, self.std, b + 1)
                e.reciprocal(lnv[:, 0, :], lnv[:, 4, :]).then_inc(self.ch, 1)
                until(e, self.ch, b * 6 + 6)
                until(e, self.tr, b * NHALF)
                for c in range(NC):
                    ins = e.tensor_scalar(xn[:, c, :], x_sb[:, bass.ds(b * NC + c, 1), :].rearrange("p o d -> p (o d)"),
                                          lnv[:, 2, c:c + 1], lnv[:, 0, c:c + 1], ALU.subtract, ALU.mult)
                    if c % CPH == CPH - 1:
                        ins.then_inc(self.xn, 1)

            def scalar_std(self, e, b):
                xn, xnT, stats, lnv = self.buffers
                until(e, self.var, b + 1)
                e.activation(lnv[:, 4, :], lnv[:, 3, :], ACT.Sqrt).then_inc(self.std, 1)

            def tensor(self, e, b):
                xn, xnT, stats, lnv = self.buffers
                until(e, self.ev, b * NHALF)
                for h in range(NHALF):
                    until(e, self.xn, b * NHALF + h + 1)
                    for c in range(CPH):
                        ins = e.transpose(bank[h][:, c * P:(c + 1) * P], xn[:, h * CPH + c, :], ident[:, :])
                    ins.then_inc(self.tr, 1)

            def scalar_evac(self, e, b, free, count):
                xn, xnT, stats, lnv = self.buffers
                until(e, free, count)
                for h in range(NHALF):
                    until(e, self.tr, b * NHALF + h + 1)
                    e.activation(xnT[:, h * HALF:(h + 1) * HALF], bank[h][:, :], ACT.Copy).then_inc(self.ev, 1)

        def project(latent):
            buf, give_back = of_phase()
            ln = Norm(buf)
            xnT, cT = ln.buffers[1], buf("cT", [P, T])
            parts = buf("parts", [P, 2, 3, T], BF16)
            rparts = buf("rparts", [2 * DR, 3, T], BF16)
            resid = buf("resid", [P, 2, HALF])
            rot = buf("rot", [2 * DR, 3, HALF])
            s_mm, s_hi, s_r1, s_mid, s_lo = sem("proj"), sem("hi"), sem("resid"), sem("mid"), sem("lo")
            s_c, s_cev = sem("latent"), sem("latent_ev")
            s_rp, s_rt, s_rr, s_rhi, s_rr1, s_rmid, s_rlo = (sem(n) for n in (
                "rope", "rope_prod", "rope_rot", "rope_hi", "rope_r1", "rope_mid", "rope_lo"))
            s_v, s_vev, s_out = sem("v"), sem("v_ev"), sem("parts_out")
            wq_ = wqk[:, 0, :] if latent else wbt[:, 0, :]
            wk_ = wqk[:, 1, :] if latent else wbt[:, 1, :]
            wv_ = wa[:, 3, :] if latent else wbt[:, 2, :]
            kin = cT if latent else xnT
            NQ = 2 * NHALF
            dma_per_b = 2 + latent
            with nc.Block() as block:
                @block.tensor
                def _(e):
                    with e.Fori(0, B) as b:
                        ln.tensor(e, b)
                        until(e, ln.ev, b * NHALF + NHALF)
                        if latent:
                            until(e, s_cev, b * NHALF)
                            for h in range(NHALF):
                                e.matmul(wide[0][:, h * HALF:(h + 1) * HALF], wa[:, 1, :],
                                         xnT[:, h * HALF:(h + 1) * HALF], start=True, stop=True).then_inc(s_c, 1)
                            until(e, s_cev, b * NHALF + NHALF)
                        for n in range(NQ):
                            t, h = divmod(n, NHALF)
                            if n >= 2:
                                until(e, s_r1, b * NQ + n - 1)
                            else:
                                until(e, s_r1, b * NQ)
                            e.matmul(bank[2 + n % 2][:, :], wk_ if t else wq_,
                                     (kin if t else xnT)[:, h * HALF:(h + 1) * HALF],
                                     start=True, stop=True).then_inc(s_mm, 1)
                        if latent:
                            for h in range(NHALF):
                                until(e, s_rt, b * NHALF + h)
                                for sw in range(2):
                                    e.matmul(wide[1][0:DR, sw * HALF:(sw + 1) * HALF], wr[:, sw, :],
                                             xnT[:, h * HALF:(h + 1) * HALF], start=True, stop=True)
                                    ins = e.matmul(wide[1][DR:2 * DR, sw * HALF:(sw + 1) * HALF], wr[:, 2 + sw, :],
                                                   cT[:, h * HALF:(h + 1) * HALF], start=True, stop=True)
                                ins.then_inc(s_rp, 1)
                        until(e, s_vev, b * NHALF)
                        for h in range(NHALF):
                            for c in range(CPH):
                                at = h * CPH + c
                                ins = e.matmul(bank[h][:, c * D:(c + 1) * D], kin[:, at * P:(at + 1) * P], wv_,
                                               start=True, stop=True)
                            ins.then_inc(s_v, 1)
                        until(e, s_vev, b * NHALF + NHALF)

                @block.scalar
                def _(e):
                    with e.Fori(0, B) as b:
                        ln.scalar_std(e, b)
                        ln.scalar_evac(e, b, s_v, b * NHALF)
                        if latent:
                            for h in range(NHALF):
                                until(e, s_c, b * NHALF + h + 1)
                                e.activation(cT[:, h * HALF:(h + 1) * HALF], wide[0][:, h * HALF:(h + 1) * HALF],
                                             ACT.Copy).then_inc(s_cev, 1)
                        until(e, s_out, b * 16 * dma_per_b)
                        for n in range(NQ):
                            t, h = divmod(n, NHALF)
                            until(e, s_mm, b * NQ + n + 1)
                            e.activation(parts[:, t, 0, h * HALF:(h + 1) * HALF], bank[2 + n % 2][:, :],
                                         ACT.Copy).then_inc(s_hi, 1)
                        if latent:
                            for h in range(NHALF):
                                until(e, s_rr, b * NHALF + h + 1)
                                e.activation(rparts[:, 0, h * HALF:(h + 1) * HALF], rot[:, 0, :],
                                             ACT.Copy).then_inc(s_rhi, 1)
                        for h in range(NHALF):
                            until(e, s_v, b * NHALF + h + 1)
                            for c in range(CPH):
                                dst = v_all[:, bass.ds(b, 1), :, h * CPH + c, :].rearrange("p o g d -> p (o g) d")
                                ins = e.activation(dst, bank[h][:, c * D:(c + 1) * D].rearrange("p (g d) -> p g d", g=NG),
                                                   ACT.Copy)
                            ins.then_inc(s_vev, 1)

                @block.vector
                def _(e):
                    with e.Fori(0, B) as b:
                        ln.vector(e, b)
                        for n in range(NQ):
                            t, h = divmod(n, NHALF)
                            until(e, s_hi, b * NQ + n + 1)
                            if n >= 2:
                                until(e, s_lo, b * NQ + n - 1)
                            else:
                                until(e, s_lo, b * NQ)
                            e.tensor_tensor(resid[:, n % 2, :], bank[2 + n % 2][:, :],
                                            parts[:, t, 0, h * HALF:(h + 1) * HALF], ALU.subtract).then_inc(s_r1, 1)
                        if latent:
                            for h in range(NHALF):
                                until(e, s_rp, b * NHALF + h + 1)
                                until(e, s_rlo, b * NHALF + h)
                                cols = slice(h * HALF, (h + 1) * HALF)
                                e.tensor_tensor(rot[:, 1, :], wide[1][0:2 * DR, 0:HALF], cs[:, 0, cols], ALU.mult)
                                e.tensor_tensor(rot[:, 2, :], wide[1][0:2 * DR, HALF:2 * HALF], cs[:, 1, cols],
                                                ALU.mult).then_inc(s_rt, 1)
                                until(e, s_rt, b * NHALF + h + 1)
                                e.tensor_tensor(rot[:, 0, :], rot[:, 1, :], rot[:, 2, :], ALU.add).then_inc(s_rr, 1)
                                until(e, s_rhi, b * NHALF + h + 1)
                                e.tensor_tensor(rot[:, 1, :], rot[:, 0, :], rparts[:, 0, cols],
                                                ALU.subtract).then_inc(s_rr1, 1)

                @block.gpsimd
                def _(e):
                    with e.Fori(0, B) as b:
                        for n in range(NQ):
                            t, h = divmod(n, NHALF)
                            cols = slice(h * HALF, (h + 1) * HALF)
                            until(e, s_r1, b * NQ + n + 1)
                            passed(e)
                            e.tensor_copy(parts[:, t, 1, cols], resid[:, n % 2, :]).then_inc(s_mid, 1)
                            until(e, s_mid, b * NQ + n + 1)
                            e.tensor_tensor(parts[:, t, 2, cols], resid[:, n % 2, :], parts[:, t, 1, cols],
                                            ALU.subtract).then_inc(s_lo, 1)
                        if latent:
                            for h in range(NHALF):
                                cols = slice(h * HALF, (h + 1) * HALF)
                                until(e, s_rr1, b * NHALF + h + 1)
                                passed(e)
                                e.tensor_copy(rparts[:, 1, cols], rot[:, 1, :]).then_inc(s_rmid, 1)
                                until(e, s_rmid, b * NHALF + h + 1)
                                e.tensor_tensor(rparts[:, 2, cols], rot[:, 1, :], rparts[:, 1, cols],
                                                ALU.subtract).then_inc(s_rlo, 1)

                @block.sync
                def _(e):
                    prime(e)
                    with e.Fori(0, B) as b:
                        for t in range(2):
                            until(e, s_lo, b * NQ + (t + 1) * NHALF)
                            e.dma_start(qk_dram[t, :, bass.ds(b, 1), :, :].rearrange("n o p t -> p (o n) t"),
                                        parts[:, t, :, :]).then_inc(s_out, 16)
                        if latent:
                            until(e, s_rlo, b * NHALF + NHALF)
                            e.dma_start(rope_dram[:, bass.ds(b, 1), :, :].rearrange("n o p t -> p (o n) t"),
                                        rparts[:, :, :]).then_inc(s_out, 16)
                    until(e, s_out, B * 16 * dma_per_b)
            give_back()

        def attend(causal):
            KEXP = P if causal else RROW + 32
            scale = float((HD + (DR if causal else 0)) ** -0.5)
            stiles = [(j, qc) for j in range(GH) for qc in range(NC)]
            NS = len(stiles)
            ttiles = [(J, kc, j, max(0, (kc - J * CPH) * P) if causal else 0) for J in range(NHALF)
                      for kc in range(min(NC, (J + 1) * CPH) if causal else NC) for j in range(GH)]
            NT = len(ttiles)
            s_max_in, s_exp_in, s_row = ([sem(f"{n}{par}") for par in range(2)]
                                         for n in ("max_stack", "exp_stack", "max_rows"))
            s_s, s_sf = sem("score_tile"), sem("score_max")
            s_mt, s_m = sem("max_turned"), sem("max_split")
            s_mch = sem("split_chain")
            s_st, s_p, s_pv = sem("t_tile"), sem("p_tile"), sem("pv")
            s_o, s_oev, s_ot, s_y, s_ych = sem("o"), sem("o_ev"), sem("o_turned"), sem("y"), sem("y_chain")
            s_vs, s_z = sem("v_stage"), sem("stack_init")

            def runs(pairs, t):
                which, found = [pair[t] for pair in pairs], []
                for n, part in enumerate(which):
                    if found:
                        first, count, begin, step = found[-1]
                        if count == 1 and part >= begin:
                            found[-1] = (first, 2, begin, part - begin)
                            continue
                        if count > 1 and part == begin + count * step:
                            found[-1] = (first, count + 1, begin, step)
                            continue
                    found.append((n, 1, part, 0))
                return found

            def parts_of(rows, count, begin, step):
                if step == 0:
                    one = rows[begin:begin + 1]
                    return one.broadcast_to([count] + list(one.shape[1:]))
                return rows[begin:begin + (count - 1) * step + 1:step]

            def head_blocks(dst, first_row, pairs, t, s):
                rows = qk_dram[t].rearrange("n b (g d j) t -> n (b g) d (j t)", g=NG, j=GH)
                for n, count, begin, step in runs(pairs, t):
                    src = parts_of(rows[:, bass.ds(s, 1)].rearrange("n o d x -> n (o d) x"), count, begin, step)
                    at = first_row + n * HD
                    yield dst[at:at + count * HD, :, :].rearrange("r j t -> r (j t)"), src

            def rope_blocks(dst, first_row, pairs, t, b, heads):
                rows = rope_dram[:, bass.ds(b, 1), t * DR:(t + 1) * DR, :].rearrange("n o r t -> n (o r) t")
                for n, count, begin, step in runs(pairs, t):
                    at = first_row + n * DR
                    if not heads:
                        yield dst[at:at + count * DR, :], parts_of(rows, count, begin, step)
                        continue
                    for i in range(count):
                        src = rows[begin + i * step].rearrange("r (o t) -> r o t", o=1).broadcast_to([DR, GH, T])
                        yield dst[at + i * DR:at + (i + 1) * DR, :, :], src

            def max_loads(s, b, par, rope):
                for t, dst in ((0, q_max[par]), (1, k_max[par])):
                    yield from head_blocks(dst, NROW, MAX_PAIRS, t, s)
                    if rope:
                        yield from rope_blocks(dst, 0, MAX_PAIRS, t, b, True)

            def exp_loads(s, b, par, rope):
                for t, dst, shared in ((0, q_exp[par], q_rope[par]), (1, k_exp[par], k_rope[par])):
                    yield from head_blocks(dst, 0, PAIRS, t, s)
                    if rope:
                        yield from rope_blocks(shared, 0, ROPE_TILE, t, b, False)
                        yield from rope_blocks(dst, RROW, ROPE_REST, t, b, True)

            buf, give_back = of_phase()
            q_exp = [buf(f"q_exp{i}", [P, GH, T], BF16) for i in range(2)]
            k_exp = [buf(f"k_exp{i}", [P, GH, T], BF16) for i in range(2)]
            q_max = [buf(f"q_max{i}", [P, GH, T], BF16) for i in range(2)]
            k_max = [buf(f"k_max{i}", [P, GH, T], BF16) for i in range(2)]
            q_rope = [buf(f"q_rope{i}", [P, T], BF16) for i in range(2)]
            k_rope = [buf(f"k_rope{i}", [P, T], BF16) for i in range(2)]
            vst = [buf(f"vst{i}", [P, NC, GH, 32]) for i in range(2)]
            NPB = 4
            pT = buf("pT", [P, NPB, HALF])
            mx = [buf(f"mx{i}", [P, GH * NC]) for i in range(2)]
            nmr = buf("nmr", [GH * NC, P])
            nmp = [buf(f"nmp{i}", [GH * NC, 3, P], BF16) for i in range(2)]
            o_sb = buf("o_sb", [P, HALF])
            rsum = buf("rsum", [P, CPH, GH, 1])
            max_clear = [] if causal else [(m[par], 0, NROW) for par in range(2) for m in (q_max, k_max)]
            exp_clear = [(q_exp[par], 32, 64) for par in range(2)]
            exp_clear += [] if causal else [(m[par], RROW, KEXP) for par in range(2) for m in (q_exp, k_exp)]
            s_zm, s_zo = sem("max_init"), sem("ones_init")
            s_vz = sem("v_init")

            n_max, n_exp = ([sum(1 for _ in loads(0, 0, 0, causal and new)) * 16 for new in (True, False)]
                            for loads in (max_loads, exp_loads))

            def loaded(s, counts):
                pair = s // 2
                return (pair // 2 + 1) * counts[0] + (pair + 1) // 2 * counts[1]

            pieces = [(k, h, min(HALF, ((qc + 1) * P if causal else T) - h * HALF))
                      for k, (j, qc) in enumerate(stiles)
                      for h in range(((qc + 1) * P - 1) // HALF + 1 if causal else T // HALF)]
            first = [n for n, t in enumerate(ttiles) if t[0] == 0][-1]

            def events(with_s):
                ev, done = [], 0
                for u in range(NT):
                    ev.append(("T", u))
                    if with_s:
                        want = len(pieces) * (u + 1) // NT + (2 if u in (first, first + 1) else 0)
                        while done < min(want, len(pieces)) or (done < len(pieces) and u == NT - 1):
                            ev.append(("S", done))
                            done += 1
                        if u == 0 and done == 0:
                            ev.append(("S", 0))
                            done = 1
                    ev += {1: [("OE", 1)], 5: [("OT", 1)], 9: [("MX", 0)], first + 1: [("OE", 0)],
                           first + 5: [("OT", 0)]}.get(u, [])
                return ev

            def steps(e, prologue, body, epilogue):
                prologue(0, 0)
                prologue(1, 1)
                body(0, 0, True, True)
                body(1, 1, True, True)
                with e.Fori(1, STEPS // 2 - 1) as pair:
                    body(pair * 2, 0, True, True)
                    body(pair * 2 + 1, 1, True, True)
                body(STEPS - 2, 0, False, True)
                body(STEPS - 1, 1, False, False)
                epilogue()

            is_first = lambda s: isinstance(s, int) and s == 0

            with nc.Block() as block:
                @block.tensor
                def _(e):
                    def score(s, par, piece):
                        k, h, w = pieces[piece]
                        j, qc = stiles[k]
                        last = piece + 1 == len(pieces) or pieces[piece + 1][0] != k
                        if piece == 0:
                            until(e, s_max_in[par], loaded(s, n_max))
                        if h == 0 and not (isinstance(s, int) and s * NS + k < 2):
                            until(e, s_sf, s * NS + k - 1)
                        diag = causal and last
                        ins = e.matmul(wide[k % 2][:, h * HALF:h * HALF + w],
                                       q_max[par][0:KMAX, j, qc * P:(qc + 1) * P],
                                       k_max[par][0:KMAX, j, h * HALF:h * HALF + w], start=True, stop=not diag)
                        if diag:
                            ins = e.matmul(wide[k % 2][:, h * HALF + w - P:h * HALF + w], identb[:, :],
                                           mask_qk[:, :], start=False, stop=True)
                        if last:
                            ins.then_inc(s_s, 1)

                    def t_score(s, par, u):
                        J, kc, j, q0 = ttiles[u]
                        if u == 0:
                            until(e, s_exp_in[par], loaded(s, n_exp))
                            until(e, s_row[par], (s // 2 + 1) * 48)
                        if isinstance(s, int) and s * NT + u < 2:
                            pass
                        else:
                            until(e, s_p, s * NT + u - 1)
                        dst = bank[u % 2][:, q0:HALF]
                        keys = slice(kc * P, (kc + 1) * P)
                        qs = slice(J * HALF + q0, (J + 1) * HALF)
                        if causal:
                            e.matmul(dst, k_rope[par][:, keys], q_rope[par][:, qs], start=True, stop=False)
                        diag = causal and kc >= J * CPH
                        ins = e.matmul(dst, k_exp[par][0:KEXP, j, keys], q_exp[par][0:KEXP, j, qs],
                                       start=not causal, stop=not diag)
                        if diag:
                            ins = e.matmul(bank[u % 2][:, q0:q0 + P], identb[:, :], mask_kq[:, :],
                                           start=False, stop=True)
                        ins.then_inc(s_st, 1)

                    def weigh(s, par, u):
                        J, kc, j, q0 = ttiles[u]
                        if u == 0:
                            until(e, s_vz, 4)
                            until(e, s_vs, s + 1)
                        if u in (0, first + 1):
                            until(e, s_oev, s * NHALF + J)
                        until(e, s_p, s * NT + u + 1)
                        last = kc == (min(NC, (J + 1) * CPH) if causal else NC) - 1
                        ins = e.matmul(bank[2][32 * j:32 * (j + 1), q0:HALF], vst[par][:, kc, j, :],
                                       pT[:, u % NPB, q0:HALF], start=(kc == 0), stop=last,
                                       tile_position=(0, 32 * j), skip_group_check=True)
                        ins.then_inc(s_pv, 1)

                    def turn_max(s, par):
                        until(e, s_sf, (s + 1) * NS)
                        until(e, s_y, s * NHALF if isinstance(s, int) and s < 1 else (s - 1) * NHALF)
                        e.transpose(bank[3][0:GH * NC, 0:P], mx[par][:, :], ident[:, :]).then_inc(s_mt, 1)

                    def turn_out(s, J, splits):
                        until(e, s_oev, s * NHALF + J + 1)
                        until(e, s_y, s * NHALF + J)
                        until(e, s_m, splits)
                        for c in range(CPH):
                            ins = e.transpose(bank[3][:, c * P:(c + 1) * P], o_sb[:, c * P:(c + 1) * P], ident[:, :])
                        ins.then_inc(s_ot, 1)

                    def prologue(s, par):
                        for piece in range(len(pieces)):
                            score(s, par, piece)
                        if s == 0:
                            turn_max(0, 0)
                        else:
                            t_score(0, 0, 0)
                            t_score(0, 0, 1)

                    def body(s, par, with_s, with_mx):
                        for what, n in events(with_s):
                            if what == "S":
                                score(s + 2, par, n)
                            elif what == "T":
                                if n + 2 < NT:
                                    t_score(s, par, n + 2)
                                elif with_mx:
                                    t_score(s + 1, 1 - par, n + 2 - NT)
                                weigh(s, par, n)
                            elif what == "MX" and with_mx:
                                turn_max(s + 1, 1 - par)
                            elif what == "OT" and n == 0:
                                turn_out(s, 0, s + 2 if with_mx else s + 1)
                            elif what == "OT" and not is_first(s):
                                turn_out(s - 1, 1, s + 1)

                    def epilogue():
                        turn_out(STEPS - 1, 1, STEPS)

                    steps(e, prologue, body, epilogue)

                @block.vector
                def _(e):
                    for par in range(2):
                        e.memset(k_exp[par][32:64, :, :], 1.0).then_inc(s_zo, 1)

                    def score(s, par, k):
                        j, qc = stiles[k]
                        n = (qc + 1) * P if causal else T
                        until(e, s_s, s * NS + k + 1)
                        if k == 0 and not (isinstance(s, int) and s < 2):
                            until(e, s_mt, s - 1)
                        e.tensor_reduce(mx[par][:, j * NC + qc:j * NC + qc + 1], wide[k % 2][:, 0:n], AX.X,
                                        ALU.max).then_inc(s_sf, 1)

                    def split_max(s, par):
                        until(e, s_mt, s + 1)
                        if not (isinstance(s, int) and s < 2):
                            until(e, s_row[par], s // 2 * 48)
                        src = bank[3][0:GH * NC, 0:P]
                        e.tensor_scalar(nmp[par][:, 0, :], src, -1.0, None, ALU.mult).then_inc(s_mch, 1)
                        until(e, s_mch, s * 3 + 1)
                        e.scalar_tensor_tensor(nmr[:, :], src, -1.0, nmp[par][:, 0, :], ALU.mult,
                                               ALU.subtract).then_inc(s_mch, 1)
                        until(e, s_mch, s * 3 + 2)
                        e.tensor_copy(nmp[par][:, 1, :], nmr[:, :]).then_inc(s_mch, 1)
                        until(e, s_mch, s * 3 + 3)
                        e.tensor_tensor(nmp[par][:, 2, :], nmr[:, :], nmp[par][:, 1, :], ALU.subtract).then_inc(s_m, 1)

                    def normalize(s, J):
                        until(e, s_ot, s * NHALF + J + 1)
                        o = bank[3][:, :].rearrange("p (c j r) -> p c j r", c=CPH, j=GH)
                        e.reciprocal(rsum[:, :, :, :], o[:, :, :, HD:HD + 1]).then_inc(s_ych, 1)
                        until(e, s_ych, s * NHALF + J + 1)
                        dst = y_all.rearrange("p b g c d -> p (b g) c d")[:, bass.ds(s, 1), J * CPH:(J + 1) * CPH, :]
                        e.tensor_tensor(dst.rearrange("p o c (j d) -> p (o c) j d", j=GH), o[:, :, :, 0:HD],
                                        rsum[:, :, :, :].broadcast_to([P, CPH, GH, HD]), ALU.mult).then_inc(s_y, 1)

                    def prologue(s, par):
                        for k in range(NS):
                            score(s, par, k)
                        if s == 0:
                            split_max(0, 0)

                    def body(s, par, with_s, with_mx):
                        for what, n in events(with_s):
                            if what == "S" and (n + 1 == len(pieces) or pieces[n + 1][0] != pieces[n][0]):
                                score(s + 2, par, pieces[n][0])
                            elif what == "MX" and with_mx:
                                split_max(s + 1, 1 - par)
                            elif what == "OT" and n == 0:
                                normalize(s, 0)
                            elif what == "OT" and not is_first(s):
                                normalize(s - 1, 1)

                    def epilogue():
                        normalize(STEPS - 1, 1)

                    steps(e, prologue, body, epilogue)

                @block.scalar
                def _(e):
                    def empty(s, J):
                        until(e, s_pv, s * NT + (NT if J else first + 1))
                        if not (isinstance(s, int) and s * NHALF + J == 0):
                            until(e, s_ot, s * NHALF + J)
                        e.activation(o_sb[:, :], bank[2][:, :], ACT.Copy).then_inc(s_oev, 1)

                    def body(s, par, with_s, with_mx):
                        for what, n in events(with_s):
                            if what == "T":
                                q0 = ttiles[n][3]
                                until(e, s_st, s * NT + n + 1)
                                if not (isinstance(s, int) and s * NT + n < NPB):
                                    until(e, s_pv, s * NT + n + 1 - NPB)
                                e.activation(pT[:, n % NPB, q0:HALF], bank[n % 2][:, q0:HALF], ACT.Exp,
                                             scale=scale).then_inc(s_p, 1)
                            elif what == "OE" and n == 0:
                                empty(s, 0)
                            elif what == "OE" and not is_first(s):
                                empty(s - 1, 1)

                    steps(e, lambda s, par: None, body, lambda: empty(STEPS - 1, 1))

                @block.gpsimd
                def _(e):
                    def stage_v(s, par):
                        src = v_all.rearrange("p b g c d -> p (b g) c d")[:, bass.ds(s, 1), :, :]
                        e.tensor_copy(vst[par][:, :, :, 0:HD],
                                      src.rearrange("p o c (j d) -> p (o c) j d", j=GH)).then_inc(s_vs, 1)

                    for counter, clear in ((s_zm, max_clear), (s_z, exp_clear)):
                        for n, (stack, r0, r1) in enumerate(clear):
                            e.memset(stack[r0:r1, :, :].bitcast(U32), 0).then_inc(counter, 1)
                            until(e, counter, n + 1)
                    for n, v in enumerate(vst):
                        e.memset(v[:, :, :, :], 0.0).then_inc(s_vz, 1)
                        until(e, s_vz, n + 1)
                    for n, v in enumerate(vst):
                        e.memset(v[:, :, :, HD:HD + 1], 1.0).then_inc(s_vz, 1)
                        until(e, s_vz, n + 3)
                    stage_v(0, 0)
                    stage_v(1, 1)
                    with e.Fori(0, STEPS // 2 - 1) as pair:
                        s = pair * 2
                        for par in range(2):
                            until(e, s_pv, (s + par + 1) * NT)
                            passed(e)
                            stage_v(s + par + 2, par)

                @block.sync
                def _(e):
                    prime(e)
                    def rows(s, par):
                        until(e, s_m, s + 1)
                        for i in range(3):
                            dst = q_exp[par][MROW + i:MROW + i + 1, :, :].rearrange("o j (c q) -> o (j c) q", q=P)
                            e.dma_start(dst, nmp[par][:, i, :]).then_inc(s_row[par], 16)

                    def load(loads, semaphore, s, b, par, new):
                        for dst, src in loads(s, b, par, causal and new):
                            e.dma_start(dst, src).then_inc(semaphore[par], 16)

                    until(e, s_zm, len(max_clear))
                    for par in range(2):
                        load(max_loads, s_max_in, par, 0, par, True)
                    until(e, s_z, len(exp_clear))
                    until(e, s_zo, 2)
                    for par in range(2):
                        load(exp_loads, s_exp_in, par, 0, par, True)
                    rows(0, 0)

                    def next_max(b, g):
                        s = b * NG + g
                        until(e, s_sf, (s + 2) * NS)
                        load(max_loads, s_max_in, s + 3, b + (g + 3) // NG, (g + 3) % 2, (g + 3) % NG < 2)

                    def follow(b, g, last):
                        s, par = b * NG + g, g % 2
                        if not (last and g == 3):
                            rows(s + 1, 1 - par)
                        if not (last and g >= 1):
                            next_max(b, g)
                        if not (last and g >= 2):
                            until(e, s_st, (s + 1) * NT)
                            load(exp_loads, s_exp_in, s + 2, b + g // 2, par, g >= 2)

                    until(e, s_sf, NS)
                    load(max_loads, s_max_in, 2, 0, 0, False)
                    with e.Fori(0, B - 1) as b:
                        for g in range(NG):
                            follow(b, g, False)
                    for g in range(NG):
                        follow(B - 1, g, True)
                    for par in range(2):
                        until(e, s_row[par], STEPS // 2 * 48)
            give_back()

        def add_projected():
            buf, give_back = of_phase()
            stage = buf("stage", [P, NC, D])
            stT = buf("stT", [P, T])
            s_g, s_t, s_tev, s_mm, s_add = sem("gathered"), sem("turned"), sem("turned_ev"), sem("o_proj"), sem("added")
            with nc.Block() as block:
                @block.sync
                def _(e):
                    prime(e)

                @block.gpsimd
                def _(e):
                    with e.Fori(0, B) as b:
                        until(e, s_t, b * NHALF)
                        passed(e)
                        for g in range(NG):
                            src = y_all[:, bass.ds(b, 1), g, :, :].rearrange("p o c d -> p (o c) d")
                            ins = e.tensor_copy(stage[:, :, g * 32:(g + 1) * 32], src)
                        ins.then_inc(s_g, 1)

                @block.tensor
                def _(e):
                    with e.Fori(0, B) as b:
                        until(e, s_g, b + 1)
                        for h in range(NHALF):
                            for c in range(CPH):
                                ins = e.transpose(bank[h][:, c * P:(c + 1) * P], stage[:, h * CPH + c, :], ident[:, :])
                            ins.then_inc(s_t, 1)
                        until(e, s_add, b * NHALF)
                        for h in range(NHALF):
                            until(e, s_tev, b * NHALF + h + 1)
                            for c in range(CPH):
                                at = h * CPH + c
                                ins = e.matmul(bank[2 + h][:, c * P:(c + 1) * P], stT[:, at * P:(at + 1) * P],
                                               wa[:, 4, :], start=True, stop=True)
                            ins.then_inc(s_mm, 1)

                @block.scalar
                def _(e):
                    with e.Fori(0, B) as b:
                        until(e, s_mm, b * NHALF)
                        for h in range(NHALF):
                            until(e, s_t, b * NHALF + h + 1)
                            e.activation(stT[:, h * HALF:(h + 1) * HALF], bank[h][:, :], ACT.Copy).then_inc(s_tev, 1)

                @block.vector
                def _(e):
                    with e.Fori(0, B) as b:
                        for h in range(NHALF):
                            until(e, s_mm, b * NHALF + h + 1)
                            rows = x_sb[:, bass.ds(b * NC + h * CPH, CPH), :]
                            e.tensor_tensor(rows, bank[2 + h][:, :].rearrange("p (c d) -> p c d", c=CPH), rows,
                                            ALU.add).then_inc(s_add, 1)
            give_back()

        def add_plain():
            with nc.Block() as block:
                @block.vector
                def _(e):
                    with e.Fori(0, B) as b:
                        for g in range(NG):
                            rows = x_sb[:, bass.ds(b * NC, NC), g * 32:(g + 1) * 32]
                            y = y_all[:, bass.ds(b, 1), g, :, :].rearrange("p o c d -> p (o c) d")
                            e.tensor_tensor(rows, rows, y, ALU.add)

        def route():
            buf, give_back = of_phase()
            ln = Norm(buf)
            xn, xnT = ln.buffers[0:2]
            s_lg, s_lev, s_out = sem("logits"), sem("logits_ev"), sem("rows_out")
            with nc.Block() as block:
                @block.sync
                def _(e):
                    prime(e)
                    with e.Fori(0, B) as b:
                        until(e, ln.xn, b * NHALF + NHALF)
                        e.dma_start(xn_dram[bass.ds(b * T, T), :].rearrange("(c p) d -> p c d", p=P),
                                    xn[:, :, :]).then_inc(s_out, 16)
                    until(e, s_out, B * 16)

                @block.tensor
                def _(e):
                    with e.Fori(0, B) as b:
                        ln.tensor(e, b)
                        until(e, ln.ev, b * NHALF + NHALF)
                        until(e, s_lev, b)
                        for c in range(NC):
                            ins = e.matmul(bank[2][:, c * NE:(c + 1) * NE], xnT[:, c * P:(c + 1) * P], rwt[:, :],
                                           start=True, stop=True)
                        ins.then_inc(s_lg, 1)

                @block.scalar
                def _(e):
                    with e.Fori(0, B) as b:
                        ln.scalar_std(e, b)
                        ln.scalar_evac(e, b, s_lg, b)

                @block.vector
                def _(e):
                    with e.Fori(0, B) as b:
                        until(e, s_out, b * 16)
                        ln.vector(e, b)
                        until(e, s_lg, b + 1)
                        e.tensor_copy(sc[:, :, bass.ds(b, 1), :].rearrange("p c o e -> p (c o) e"),
                                      bank[2][:, 0:NC * NE].rearrange("p (c e) -> p c e", c=NC)).then_inc(s_lev, 1)
            give_back()

        def choose():
            buf, give_back = of_phase()
            scm = buf("scm", [P, NC, B])
            work = buf("work", [B * NE, T])
            cand = buf("cand", [B * NE, T])
            top8 = buf("top8", [B * NE, 8])
            topc = buf("topc", [B * NE, 1])
            lastv = buf("lastv", [B * NE, 3])
            mask = buf("mask", [B * NE, T])
            gres = buf("gres", [P, NC, B * NE])
            s_v, s_a, s_t, s_g = sem("choose_v"), sem("choose_exp"), sem("scores_turned"), sem("gates_turned")
            s_gt = sem("gates_back")
            with nc.Block() as block:
                @block.sync
                def _(e):
                    prime(e)

                @block.vector
                def _(e):
                    n = [0]

                    def then(ins):
                        n[0] += 1
                        ins.then_inc(s_v, 1)
                        until(e, s_v, n[0])

                    rows = sc.rearrange("p c b e -> p (c b) e")
                    m = scm.rearrange("p c b -> p (c b)")
                    mb = scm.rearrange("p c (b o) -> p (c b) o", o=1).broadcast_to([P, NC * B, NE])
                    then(e.tensor_reduce(m, rows, AX.X, ALU.max))
                    then(e.tensor_tensor(rows, rows, mb, ALU.subtract))
                    until(e, s_a, 1)
                    then(e.tensor_reduce(m, rows, AX.X, ALU.add))
                    then(e.reciprocal(m, m))
                    then(e.tensor_tensor(rows, rows, mb, ALU.mult))
                    until(e, s_t, 1)
                    e.tensor_copy(scT[:, :], wide[0][0:B * NE, :])
                    then(e.tensor_copy(work[:, :], wide[0][0:B * NE, :]))
                    base = n[0]
                    with e.Fori(0, ROUNDS) as r:
                        e.max(top8[:, :], work[:, :]).then_inc(s_v, 1)
                        until(e, s_v, r * 2 + base + 1)
                        passed(e)
                        e.match_replace(work[:, :], top8[:, :], work[:, :], -1.0).then_inc(s_v, 1)
                        until(e, s_v, r * 2 + base + 2)
                    n[0] += 2 * ROUNDS
                    then(e.max(top8[:, :], work[:, :]))
                    e.tensor_copy(last_gate[:, :], top8[:, 0:1])
                    then(e.scalar_tensor_tensor(cand[:, :], work[:, :], top8[:, 0:1], rev[:, :], ALU.is_equal, ALU.mult))
                    then(e.tensor_reduce(topc[:, :], cand[:, :], AX.X, ALU.max))
                    then(e.tensor_scalar(lastv[:, 0:1], topc[:, :], -1.0, float(T), ALU.mult, ALU.add))
                    then(e.tensor_tensor(lastv[:, 1:2], lastv[:, 0:1], first_row[:, :], ALU.add))
                    e.tensor_copy(last_tok[:, :], lastv[:, 1:2])
                    then(e.tensor_tensor(lastv[:, 2:3], lastv[:, 1:2], spare[:, :], ALU.subtract))
                    e.tensor_scalar(last_to[:, :], own[:, :], lastv[:, 2:3], spare[:, 0:1], ALU.mult, ALU.add)
                    then(e.tensor_scalar(mask[:, :], work[:, :], 0.0, None, ALU.is_lt))
                    then(e.tensor_tensor_scan(work[:, :], mask[:, :], mask[:, :], 0.0, ALU.add, ALU.max))
                    e.tensor_tensor(work[:, :], work[:, :], mask[:, :], ALU.mult).then_inc(s_g, 1)
                    then(e.tensor_scalar(cand[:, :], cand[:, :], topc[:, 0:1], None, ALU.is_equal))
                    then(e.tensor_tensor(cand[:, :], cand[:, :], mask[:, :], ALU.add))
                    e.tensor_tensor(scT[:, :], scT[:, :], cand[:, :], ALU.mult).then_inc(s_g, 1)
                    until(e, s_gt, 1)
                    e.tensor_scalar(slot_of.rearrange("p c r -> p (c r)"), bank[1][:, 0:NC * B * NE], -1.0, None, ALU.add)
                    until(e, s_gt, 2)
                    gates = bank[0][:, 0:NC * B * NE].rearrange("p (c r) -> p c r", c=NC)
                    then(e.tensor_copy(facts[:, :, :, 2], gates))
                    then(e.tensor_tensor(gres[:, :, :], gates, facts[:, :, :, 2], ALU.subtract))
                    then(e.tensor_copy(facts[:, :, :, 3], gres[:, :, :]))
                    e.tensor_tensor(facts[:, :, :, 4], gres[:, :, :], facts[:, :, :, 3], ALU.subtract)

                @block.scalar
                def _(e):
                    rows = sc.rearrange("p c b e -> p (c b e)")
                    until(e, s_v, 2)
                    e.activation(rows, rows, ACT.Exp).then_inc(s_a, 1)

                @block.tensor
                def _(e):
                    until(e, s_v, 5)
                    for c in range(NC):
                        ins = e.transpose(wide[0][0:B * NE, c * P:(c + 1) * P],
                                          sc[:, c, :, :].rearrange("p b e -> p (b e)"), ident[:, :])
                    ins.then_inc(s_t, 1)
                    for n, (to, rows) in enumerate(((bank[1], work), (bank[0], scT))):
                        until(e, s_g, n + 1)
                        for c in range(NC):
                            ins = e.transpose(to[:, c * B * NE:(c + 1) * B * NE], rows[:, c * P:(c + 1) * P],
                                              ident[0:B * NE, 0:B * NE])
                        ins.then_inc(s_gt, 1)
            give_back()

        def experts(last):
            buf, give_back = of_phase()
            two = range(2)
            w1b = [buf(f"w1b{i}", [P, HID]) for i in two]
            w2b = [buf(f"w2b{i}", [P, KH, D]) for i in two]
            picks = [buf(f"picks{b}", [P, NC, 2 * P], BF16) for b in range(B)]
            idxf = buf("idxf", [P, NM])
            gpart = buf("gpart", [P, NM])
            fsb = buf("fsb", [P, NM, NFACT])
            s_ch = sem("gate_chain")
            idx = [buf(f"idx{i}", [P, NM], U32) for i in two]
            gsl = [buf(f"gsl{i}", [P, NM]) for i in two]
            idl = [buf(f"idl{i}", [B * NE, 1], U32) for i in two]
            xg = [buf(f"xg{i}", [P, NM, D]) for i in two]
            yg = [buf(f"yg{i}", [P, NM, D]) for i in two]
            yl = [buf(f"yl{i}", [B * NE, D]) for i in two]
            xgT = buf("xgT", [P, NM * P])
            hT = buf("hT", [P, KH, NM * P])
            xl = buf("xl", [B * NE, D])
            xlT = buf("xlT", [P, B * NE])
            hl = buf("hl", [P, KH, B * NE])
            zero = buf("zero", [B * NE, D])
            s_b, s_bx, s_z = sem("bias"), sem("bias_added"), sem("zeroed")
            s_base, s_w = sem("base_out"), [sem(f"weights{i}") for i in two]
            s_pick, s_pk, s_f, s_ix = sem("picks"), sem("picks_read"), sem("slot_facts"), sem("indices")
            s_g, s_gl, s_sc = [sem(f"gathered{i}", False) for i in two], sem("last_gathered", False), sem("added", False)
            added = lambda ex: ex * (NM + 1) * 16 + 16
            s_tr, s_xev, s_h, s_a = sem("turned"), sem("turned_ev"), sem("hidden"), sem("gelu")
            s_hl, s_al, s_y, s_yev = sem("hidden_last"), sem("gelu_last"), sem("expert_out"), sem("gated")
            s_yl, s_ylev, s_lt, s_ltev = sem("last_out"), sem("last_gated"), sem("last_turned"), sem("last_ev")
            s_back = sem("back")
            NHB = 2 * KH
            facts_ps = wide[1][:, 0:NM * 8].rearrange("p (m f) -> p m f", f=8)
            hl_ps = wide[1][:, HALF:HALF + KH * B * NE]
            yl_ps = wide[1][0:B * NE, HALF + P:HALF + 2 * P]
            rows_of = lambda ap: ap[0:B * T, :].rearrange("(n p) d -> p n d", p=P)

            def run(e, body):
                with e.Fori(0, NE // 2 - 1) as pair:
                    for par in two:
                        body(pair * 2 + par, par, True, True)
                body(NE - 2, 0, False, True)
                body(NE - 1, 1, False, False)

            with nc.Block() as block:
                @block.sync
                def _(e):
                    prime(e)

                    def weights(ex, par):
                        e.dma_start(w1b[par][:, :], w1[bass.ds(ex, 1)].rearrange("o p h -> (o p) h")).then_inc(s_w[par], 16)
                        e.dma_start(w2b[par][:, :, :], w2[bass.ds(ex, 1)].rearrange("o (k p) d -> p (o k) d", p=P)
                                    ).then_inc(s_w[par], 16)

                    weights(0, 0)
                    weights(1, 1)
                    until(e, s_bx, B * NHALF)
                    e.dma_start(rows_of(acc_dram), x_sb[:, :, :]).then_inc(s_base, 16)

                    def body(ex, par, ahead2, ahead1):
                        if ahead2:
                            until(e, s_yl, ex + 1)
                            weights(ex + 2, par)

                    run(e, body)
                    until(e, s_sc, added(NE))
                    if last:
                        e.dma_start(out.rearrange("b t d -> (b t) d"), acc_dram[0:B * T, :]).then_inc(s_back, 16)
                    else:
                        e.dma_start(x_sb[:, :, :], rows_of(acc_dram)).then_inc(s_back, 16)
                    until(e, s_back, 16)

                @block.gpsimd
                def _(e):
                    def gather(ex, par):
                        until(e, s_ix, ex + 1)
                        if not (isinstance(ex, int) and ex < 2):
                            until(e, s_tr, (ex - 1) * 2)
                        passed(e)
                        for m in range(NM):
                            e.indirect_dma_start(xg[par][:, m, :], None, xn_dram,
                                                 bass.IndirectOffsetOnAxis(ap=idx[par][:, m:m + 1], axis=0)
                                                 ).then_inc(s_g[par], 16)

                    e.memset(zero[:, :], 0.0).then_inc(s_z, 1)
                    until(e, s_z, 1)
                    e.dma_start(acc_dram[B * T:B * T + B * NE, :], zero[:, :]).then_inc(s_sc, 16)
                    e.indirect_dma_start(xl[:, :], None, xn_dram,
                                         bass.IndirectOffsetOnAxis(ap=last_tok[:, 0:1], axis=0)).then_inc(s_gl, 16)
                    gather(0, 0)
                    until(e, s_base, 16)

                    def body(ex, par, ahead2, ahead1):
                        if ahead1:
                            gather(ex + 1, 1 - par)
                        until(e, s_sc, added(ex))
                        for m in range(NM):
                            if m % CPH == 0:
                                until(e, s_yev, ex * 2 + m // CPH + 1)
                                passed(e)
                            e.indirect_dma_start(acc_dram, bass.IndirectOffsetOnAxis(ap=idx[par][:, m:m + 1], axis=0),
                                                 yg[par][:, m, :], None, compute_op=ALU.add).then_inc(s_sc, 16)
                        until(e, s_ylev, ex + 1)
                        passed(e)
                        e.indirect_dma_start(acc_dram, bass.IndirectOffsetOnAxis(ap=idl[par][:, 0:1], axis=0),
                                             yl[par][:, :], None, compute_op=ALU.add).then_inc(s_sc, 16)

                    run(e, body)

                @block.tensor
                def _(e):
                    def read_slots(ex):
                        for b in range(B):
                            until(e, s_pick, ex * B + b + 1)
                            if b == 0:
                                until(e, s_f, ex)
                            for h in two:
                                for c in range(NC):
                                    ins = e.matmul(facts_ps[:, b * 2 + h, 0:NFACT], picks[b][:, c, h * P:(h + 1) * P],
                                                   facts[:, c, bass.ds(b * NE + ex, 1), :].rearrange("p o f -> p (o f)"),
                                                   start=(c == 0), stop=(c == NC - 1))
                            ins.then_inc(s_pk, 1)

                    for b in range(B):
                        for h in range(NHALF):
                            until(e, s_bx, max(0, b * NHALF + h - 1))
                            for c in range(CPH):
                                at = h * CPH + c
                                ins = e.matmul(bank[2 + h][:, c * D:(c + 1) * D],
                                               scT[:, at * P:(at + 1) * P], b2blk[:, b, :], start=True, stop=True)
                            ins.then_inc(s_b, 1)
                    read_slots(0)
                    read_slots(1)
                    until(e, s_bx, B * NHALF)
                    until(e, s_gl, 16)
                    e.transpose(hl_ps[:, 0:B * NE], xl[:, :], ident[0:B * NE, 0:B * NE]).then_inc(s_lt, 1)

                    def body(ex, par, ahead2, ahead1):
                        until(e, s_g[par], (ex // 2 + 1) * NM * 16)
                        until(e, s_xev, ex * 2)
                        for h in two:
                            for c in range(CPH):
                                ins = e.transpose(bank[h][:, c * P:(c + 1) * P], xg[par][:, h * CPH + c, :], ident[:, :])
                            ins.then_inc(s_tr, 1)
                        until(e, s_w[par], (ex // 2 + 1) * 32)
                        for n in range(NHB):
                            J, k = divmod(n, KH)
                            if k == 0:
                                until(e, s_xev, ex * 2 + J + 1)
                            if not (isinstance(ex, int) and ex * NHB + n < 2):
                                until(e, s_a, ex * NHB + n - 1)
                            e.matmul(wide[0][:, (n % 2) * HALF:(n % 2 + 1) * HALF], w1b[par][:, k * P:(k + 1) * P],
                                     xgT[:, J * HALF:(J + 1) * HALF], start=True, stop=True).then_inc(s_h, 1)
                        until(e, s_ltev, 1)
                        until(e, s_ylev, ex)
                        for k in range(KH):
                            ins = e.matmul(hl_ps[:, k * B * NE:(k + 1) * B * NE], w1b[par][:, k * P:(k + 1) * P],
                                           xlT[:, :], start=True, stop=True)
                        ins.then_inc(s_hl, 1)
                        if ahead2:
                            read_slots(ex + 2)
                        for J in two:
                            until(e, s_a, ex * NHB + (J + 1) * KH)
                            until(e, s_yev, ex * 2 + J - 1 if isinstance(ex, int) and ex == 0 and J == 1 else
                                  (ex * 2 - 1 + J if not (isinstance(ex, int) and ex == 0) else 0))
                            for c in range(CPH):
                                m = J * CPH + c
                                for k in range(KH):
                                    ins = e.matmul(bank[2 + J][:, c * P:(c + 1) * P], hT[:, k, m * P:(m + 1) * P],
                                                   w2b[par][:, k, :], start=(k == 0), stop=(k == KH - 1))
                            ins.then_inc(s_y, 1)
                        until(e, s_al, ex + 1)
                        for k in range(KH):
                            ins = e.matmul(yl_ps, hl[:, k, :], w2b[par][:, k, :], start=(k == 0), stop=(k == KH - 1))
                        ins.then_inc(s_yl, 1)

                    run(e, body)

                @block.scalar
                def _(e):
                    until(e, s_lt, 1)
                    e.activation(xlT[:, :], hl_ps[:, 0:B * NE], ACT.Copy).then_inc(s_ltev, 1)

                    def body(ex, par, ahead2, ahead1):
                        until(e, s_h, ex * NHB)
                        for h in two:
                            until(e, s_tr, ex * 2 + h + 1)
                            e.activation(xgT[:, h * HALF:(h + 1) * HALF], bank[h][:, :], ACT.Copy).then_inc(s_xev, 1)
                        for n in range(NHB):
                            J, k = divmod(n, KH)
                            if k == 0:
                                until(e, s_y, max(0, ex * 2 - 1 + J) if isinstance(ex, int) else ex * 2 - 1 + J)
                            until(e, s_h, ex * NHB + n + 1)
                            passed(e)
                            e.activation(hT[:, k, J * HALF:(J + 1) * HALF], wide[0][:, (n % 2) * HALF:(n % 2 + 1) * HALF],
                                         ACT.Gelu, bias=b1t[:, bass.ds(ex * KH + k, 1)]).then_inc(s_a, 1)
                        until(e, s_hl, ex + 1)
                        until(e, s_yl, ex)
                        passed(e)
                        for k in range(KH):
                            ins = e.activation(hl[:, k, :], hl_ps[:, k * B * NE:(k + 1) * B * NE],
                                               ACT.Gelu, bias=b1t[:, bass.ds(ex * KH + k, 1)])
                        ins.then_inc(s_al, 1)

                    run(e, body)

                @block.vector
                def _(e):
                    def pick(ex):
                        for b in range(B):
                            if not (isinstance(ex, int) and ex == 0):
                                until(e, s_pk, (ex - 1) * B + b + 1)
                            for c in range(NC):
                                ins = e.tensor_scalar(picks[b][:, c, :], slots[:, :],
                                                      slot_of[:, c, bass.ds(b * NE + ex, 1)], None, ALU.is_equal)
                            ins.then_inc(s_pick, 1)

                    def index(ex, par):
                        until(e, s_pk, (ex + 1) * B)
                        e.tensor_copy(fsb[:, :, :], facts_ps[:, :, 0:NFACT]).then_inc(s_f, 1)
                        until(e, s_f, ex + 1)
                        e.tensor_tensor(idxf[:, :], fsb[:, :, 0], fsb[:, :, 1], ALU.add).then_inc(s_ch, 1)
                        e.tensor_tensor(gpart[:, :], fsb[:, :, 2], fsb[:, :, 3], ALU.add).then_inc(s_ch, 1)
                        until(e, s_ch, ex * 2 + 2)

                    def publish(ex, par):
                        if not (isinstance(ex, int) and ex < 2):
                            until(e, s_sc, added(ex - 1))
                        e.tensor_copy(idl[par][:, :], last_to[:, bass.ds(ex, 1)])
                        e.tensor_tensor(gsl[par][:, :], gpart[:, :], fsb[:, :, 4], ALU.add)
                        e.tensor_copy(idx[par][:, :], idxf[:, :]).then_inc(s_ix, 1)

                    pick(0)
                    for b in range(B):
                        for h in range(NHALF):
                            until(e, s_b, b * NHALF + h + 1)
                            rows = x_sb[:, b * NC + h * CPH:b * NC + (h + 1) * CPH, :]
                            e.tensor_tensor(rows, bank[2 + h][:, :].rearrange("p (c d) -> p c d", c=CPH),
                                            rows, ALU.add).then_inc(s_bx, 1)
                    index(0, 0)
                    publish(0, 0)
                    pick(1)
                    index(1, 1)
                    publish(1, 1)

                    def body(ex, par, ahead2, ahead1):
                        if ahead2:
                            pick(ex + 2)
                            index(ex + 2, par)
                        until(e, s_ix, ex + 1)
                        for J in two:
                            until(e, s_y, ex * 2 + J + 1)
                            for c in range(CPH):
                                m = J * CPH + c
                                ins = e.tensor_scalar(yg[par][:, m, :], bank[2 + J][:, c * P:(c + 1) * P],
                                                      gsl[par][:, m:m + 1], None, ALU.mult)
                            ins.then_inc(s_yev, 1)
                        until(e, s_yl, ex + 1)
                        e.tensor_scalar(yl[par][:, :], yl_ps, last_gate[:, 0:1], None, ALU.mult).then_inc(s_ylev, 1)
                        if ahead2:
                            publish(ex + 2, par)

                    run(e, body)
            give_back()

        load()
        project(True)
        attend(True)
        add_projected()
        route()
        choose()
        experts(False)
        project(False)
        attend(False)
        add_plain()
        route()
        choose()
        experts(True)


_INS = ["L0_attn_a_x", "L0_attn_a_W_kv_down", "L0_attn_a_W_k_up", "L0_attn_a_W_v_up", "L0_attn_a_W_q",
        "L0_attn_a_W_q_rope", "L0_attn_a_W_k_rope", "L0_attn_a_W_o", "L0_attn_b_Wq", "L0_attn_b_Wk",
        "L0_attn_b_Wv", "L0_ffn_router_w", "L0_ffn_w1", "L0_ffn_b1", "L0_ffn_w2", "L0_ffn_b2"]


def rope_tables():
    import numpy as np
    inv = (1.0 / 10000.0 ** (np.arange(0, DR, 2, dtype=np.float32) / np.float32(DR))).astype(np.float32)
    ang = np.outer(inv, np.arange(T, dtype=np.float32)).astype(np.float32)
    c, s = np.cos(ang).astype(np.float32), np.sin(ang).astype(np.float32)
    return np.concatenate([c, c], 0), np.concatenate([-s, s], 0)


def kernel(**inputs):
    import numpy as np
    import concourse.bacc as bacc
    from concourse.bass_utils import run_bass_kernel_spmd as run

    nc = bacc.Bacc("TRN2", target_bir_lowering=False, num_devices=1)
    arrays, args = {}, []
    named = [(n, np.ascontiguousarray(inputs[n])) for n in _INS]
    named += list(zip(("rope_cos", "rope_sin"), rope_tables()))
    for name, a in named:
        arrays[f"in_{name}"] = a
        args.append(nc.dram_tensor(f"in_{name}", a.shape, mybir.dt.from_np(a.dtype), kind="ExternalInput").ap())
    args.append(nc.dram_tensor("out_0", (B, T, D), F32, kind="ExternalOutput").ap())
    mk_program(nc, *args)
    r = run(nc, [arrays], core_ids=[0])
    return r.results[0]["out_0"]
```
